# Optimizing a Trainium2 kernel written in Bass

```python
import numpy as np
import jax
import jax.numpy as jnp

def _softmax(x, axis=-1):
    return jax.nn.softmax(x, axis=axis)

def _gelu(x):
    return jax.nn.gelu(x, approximate=True)

def _silu(x):
    return jax.nn.silu(x)

def _sigmoid(x):
    return jax.nn.sigmoid(x)

def _layernorm(x, axis=-1, eps=1e-05):
    m = jnp.mean(x, axis=axis, keepdims=True)
    v = jnp.var(x, axis=axis, keepdims=True)
    return (x - m) / jnp.sqrt(v + eps)

def _scatter_add(tgt, idx, src, axis=0):
    return tgt.at[idx].add(src)

def _segment_sum(src, seg, n):
    return jax.ops.segment_sum(src, seg, n)
kernel_name = 'mk_sandwich_d1_jaxref_r8_b5bc90'

def setup_inputs(seed: int=0):
    np.random.seed(seed)
    _w = jnp.asarray

    def _L0_attn_setup():
        import jax, jax.numpy as jnp
        from jax import lax
        import numpy as np
        B, T, C = (8, 128, 128)
        H = 4 * C
        TAU, VTH, ATAN_ALPHA = (2.0, 1.0, 2.0)

        @jax.custom_vjp
        def spike(x):
            return (x >= 0).astype(x.dtype)

        def _spike_fwd(x):
            return ((x >= 0).astype(x.dtype), x)

        def _spike_bwd(x, g):
            sg = ATAN_ALPHA / (2.0 * (1.0 + (jnp.pi / 2.0 * ATAN_ALPHA * x) ** 2))
            return (g * sg,)
        spike.defvjp(_spike_fwd, _spike_bwd)

        def layer_norm(x, s, b, eps=1e-05):
            m = jnp.mean(x, -1, keepdims=True)
            v = jnp.var(x, -1, keepdims=True)
            return (x - m) * lax.rsqrt(v + eps) * s + b

        def time_shift(x):
            return jnp.pad(x, ((0, 0), (1, 0), (0, 0)))[:, :-1]

        def wkv(w_decay, u, k, v):
            W = -jnp.exp(w_decay)
            kT = jnp.swapaxes(k, 0, 1)
            vT = jnp.swapaxes(v, 0, 1)
            p0 = jnp.zeros_like(kT[0])
            q0 = jnp.zeros_like(kT[0])
            o0 = jnp.full_like(kT[0], -1e+38)

            def step(carry, kv_t):
                p, q, o = carry
                kt, vt = kv_t
                no = jnp.maximum(o, u + kt)
                A = jnp.exp(o - no)
                Bc = jnp.exp(u + kt - no)
                y = (A * p + Bc * vt) / (A * q + Bc)
                no2 = jnp.maximum(W + o, kt)
                A2 = jnp.exp(W + o - no2)
                B2 = jnp.exp(kt - no2)
                return ((A2 * p + B2 * vt, A2 * q + B2, no2), y)
            _, ys = lax.scan(step, (p0, q0, o0), (kT, vT))
            return jnp.swapaxes(ys, 0, 1)

        def lif(x):
            xT = jnp.swapaxes(x, 0, 1)

            def step(v, xt):
                v = v + (xt - v) / TAU
                s = spike(v - VTH)
                return (v * (1.0 - s), s)
            _, sT = lax.scan(step, jnp.zeros_like(xT[0]), xT)
            return jnp.swapaxes(sT, 0, 1)

        def time_mix(x, tmk, tmv, tmr, w_decay, u_first, Wk, Wv, Wr, Wo):
            xx = time_shift(x)
            xk = x * tmk + xx * (1.0 - tmk)
            xv = x * tmv + xx * (1.0 - tmv)
            xr = x * tmr + xx * (1.0 - tmr)
            k = xk @ Wk
            v = xv @ Wv
            sr = jax.nn.sigmoid(xr @ Wr)
            return sr * wkv(w_decay, u_first, k, v) @ Wo

        def channel_mix(x, tmk, tmr, Wk, Wr, Wv):
            xx = time_shift(x)
            xk = x * tmk + xx * (1.0 - tmk)
            xr = x * tmr + xx * (1.0 - tmr)
            k = jnp.square(jax.nn.relu(xk @ Wk))
            return jax.nn.sigmoid(xr @ Wr) * (k @ Wv)
        key = jax.random.key(seed)
        ks = jax.random.split(key, 20)
        rn = lambda i, shape, s=1.0: s * jax.random.normal(ks[i], shape, dtype=jnp.float32)
        ru = lambda i, shape: jax.random.uniform(ks[i], shape, dtype=jnp.float32)
        return dict(x=rn(0, (B, T, C)), ln1_s=jnp.ones((C,), jnp.float32), ln1_b=jnp.zeros((C,), jnp.float32), ln2_s=jnp.ones((C,), jnp.float32), ln2_b=jnp.zeros((C,), jnp.float32), tmk=ru(1, (C,)), tmv=ru(2, (C,)), tmr=ru(3, (C,)), w_decay=rn(4, (C,), 0.5), u_first=rn(5, (C,), 0.5), Wk=rn(6, (C, C), 0.02), Wv=rn(7, (C, C), 0.02), Wr=rn(8, (C, C), 0.02), Wo=rn(9, (C, C), 0.02), f_tmk=ru(10, (C,)), f_tmr=ru(11, (C,)), fWk=rn(12, (C, H), 0.02), fWr=rn(13, (C, C), 0.02), fWv=rn(14, (H, C), 0.02))
    _L0_attn_in = _L0_attn_setup()

    def _L0_ffn_setup():
        import jax, jax.numpy as jnp
        import numpy as np
        D_IN, D_HID = (128, 512)

        def _ternary(key, shape):
            return jax.random.randint(key, shape, -1, 2).astype(jnp.float32)

        def _tlin(x, w, s):
            return jnp.einsum('bsi,oi->bso', x, w) * s
        key = jax.random.key(seed)
        ks = jax.random.split(key, 12)
        inv = lambda fan: 1.0 / np.sqrt(fan).astype(np.float32)
        return {'x': jax.random.normal(ks[0], (4, 256, D_IN), dtype=jnp.float32), 'w1_w': _ternary(ks[1], (D_HID, D_IN)), 'w1_s': jax.random.uniform(ks[2], (D_HID,), dtype=jnp.float32) * inv(D_IN), 'w2_w': _ternary(ks[3], (D_HID, D_IN)), 'w2_s': jax.random.uniform(ks[4], (D_HID,), dtype=jnp.float32) * inv(D_IN), 'h1_w': _ternary(ks[5], (D_HID, D_HID)), 'h1_s': jax.random.uniform(ks[6], (D_HID,), dtype=jnp.float32) * inv(D_HID), 'h2_w': _ternary(ks[7], (D_HID, D_HID)), 'h2_s': jax.random.uniform(ks[8], (D_HID,), dtype=jnp.float32) * inv(D_HID), 'w3_w': _ternary(ks[9], (D_IN, D_HID)), 'w3_s': jax.random.uniform(ks[10], (D_IN,), dtype=jnp.float32) * inv(D_HID)}
    _L0_ffn_in = _L0_ffn_setup()
    _d = {'L0_attn_x': _L0_attn_in['x'], 'L0_attn_ln1_s': _L0_attn_in['ln1_s'], 'L0_attn_ln1_b': _L0_attn_in['ln1_b'], 'L0_attn_ln2_s': _L0_attn_in['ln2_s'], 'L0_attn_ln2_b': _L0_attn_in['ln2_b'], 'L0_attn_tmk': _L0_attn_in['tmk'], 'L0_attn_tmv': _L0_attn_in['tmv'], 'L0_attn_tmr': _L0_attn_in['tmr'], 'L0_attn_w_decay': _L0_attn_in['w_decay'], 'L0_attn_u_first': _L0_attn_in['u_first'], 'L0_attn_Wk': _L0_attn_in['Wk'], 'L0_attn_Wv': _L0_attn_in['Wv'], 'L0_attn_Wr': _L0_attn_in['Wr'], 'L0_attn_Wo': _L0_attn_in['Wo'], 'L0_attn_f_tmk': _L0_attn_in['f_tmk'], 'L0_attn_f_tmr': _L0_attn_in['f_tmr'], 'L0_attn_fWk': _L0_attn_in['fWk'], 'L0_attn_fWr': _L0_attn_in['fWr'], 'L0_attn_fWv': _L0_attn_in['fWv'], 'L0_ffn_w1_w': _L0_ffn_in['w1_w'], 'L0_ffn_w1_s': _L0_ffn_in['w1_s'], 'L0_ffn_w2_w': _L0_ffn_in['w2_w'], 'L0_ffn_w2_s': _L0_ffn_in['w2_s'], 'L0_ffn_h1_w': _L0_ffn_in['h1_w'], 'L0_ffn_h1_s': _L0_ffn_in['h1_s'], 'L0_ffn_h2_w': _L0_ffn_in['h2_w'], 'L0_ffn_h2_s': _L0_ffn_in['h2_s'], 'L0_ffn_w3_w': _L0_ffn_in['w3_w'], 'L0_ffn_w3_s': _L0_ffn_in['w3_s']}
    _x0 = _d['L0_attn_x']
    _d['L0_attn_x'] = jax.random.normal(jax.random.fold_in(jax.random.key(seed), 1), (32, 256, 128), dtype=_x0.dtype)
    del _x0
    return _d

def reference(L0_attn_x, L0_attn_ln1_s, L0_attn_ln1_b, L0_attn_ln2_s, L0_attn_ln2_b, L0_attn_tmk, L0_attn_tmv, L0_attn_tmr, L0_attn_w_decay, L0_attn_u_first, L0_attn_Wk, L0_attn_Wv, L0_attn_Wr, L0_attn_Wo, L0_attn_f_tmk, L0_attn_f_tmr, L0_attn_fWk, L0_attn_fWr, L0_attn_fWv, L0_ffn_w1_w, L0_ffn_w1_s, L0_ffn_w2_w, L0_ffn_w2_s, L0_ffn_h1_w, L0_ffn_h1_s, L0_ffn_h2_w, L0_ffn_h2_s, L0_ffn_w3_w, L0_ffn_w3_s):

    def _L0_attn_ref(x, ln1_s, ln1_b, ln2_s, ln2_b, tmk, tmv, tmr, w_decay, u_first, Wk, Wv, Wr, Wo, f_tmk, f_tmr, fWk, fWr, fWv):
        import jax, jax.numpy as jnp
        from jax import lax
        import numpy as np
        B, T, C = (8, 128, 128)
        H = 4 * C
        TAU, VTH, ATAN_ALPHA = (2.0, 1.0, 2.0)

        @jax.custom_vjp
        def spike(x):
            return (x >= 0).astype(x.dtype)

        def _spike_fwd(x):
            return ((x >= 0).astype(x.dtype), x)

        def _spike_bwd(x, g):
            sg = ATAN_ALPHA / (2.0 * (1.0 + (jnp.pi / 2.0 * ATAN_ALPHA * x) ** 2))
            return (g * sg,)
        spike.defvjp(_spike_fwd, _spike_bwd)

        def layer_norm(x, s, b, eps=1e-05):
            m = jnp.mean(x, -1, keepdims=True)
            v = jnp.var(x, -1, keepdims=True)
            return (x - m) * lax.rsqrt(v + eps) * s + b

        def time_shift(x):
            return jnp.pad(x, ((0, 0), (1, 0), (0, 0)))[:, :-1]

        def wkv(w_decay, u, k, v):
            W = -jnp.exp(w_decay)
            kT = jnp.swapaxes(k, 0, 1)
            vT = jnp.swapaxes(v, 0, 1)
            p0 = jnp.zeros_like(kT[0])
            q0 = jnp.zeros_like(kT[0])
            o0 = jnp.full_like(kT[0], -1e+38)

            def step(carry, kv_t):
                p, q, o = carry
                kt, vt = kv_t
                no = jnp.maximum(o, u + kt)
                A = jnp.exp(o - no)
                Bc = jnp.exp(u + kt - no)
                y = (A * p + Bc * vt) / (A * q + Bc)
                no2 = jnp.maximum(W + o, kt)
                A2 = jnp.exp(W + o - no2)
                B2 = jnp.exp(kt - no2)
                return ((A2 * p + B2 * vt, A2 * q + B2, no2), y)
            _, ys = lax.scan(step, (p0, q0, o0), (kT, vT))
            return jnp.swapaxes(ys, 0, 1)

        def lif(x):
            xT = jnp.swapaxes(x, 0, 1)

            def step(v, xt):
                v = v + (xt - v) / TAU
                s = spike(v - VTH)
                return (v * (1.0 - s), s)
            _, sT = lax.scan(step, jnp.zeros_like(xT[0]), xT)
            return jnp.swapaxes(sT, 0, 1)

        def time_mix(x, tmk, tmv, tmr, w_decay, u_first, Wk, Wv, Wr, Wo):
            xx = time_shift(x)
            xk = x * tmk + xx * (1.0 - tmk)
            xv = x * tmv + xx * (1.0 - tmv)
            xr = x * tmr + xx * (1.0 - tmr)
            k = xk @ Wk
            v = xv @ Wv
            sr = jax.nn.sigmoid(xr @ Wr)
            return sr * wkv(w_decay, u_first, k, v) @ Wo

        def channel_mix(x, tmk, tmr, Wk, Wr, Wv):
            xx = time_shift(x)
            xk = x * tmk + xx * (1.0 - tmk)
            xr = x * tmr + xx * (1.0 - tmr)
            k = jnp.square(jax.nn.relu(xk @ Wk))
            return jax.nn.sigmoid(xr @ Wr) * (k @ Wv)
        x = x + lif(time_mix(layer_norm(x, ln1_s, ln1_b), tmk, tmv, tmr, w_decay, u_first, Wk, Wv, Wr, Wo))
        x = x + lif(channel_mix(layer_norm(x, ln2_s, ln2_b), f_tmk, f_tmr, fWk, fWr, fWv))
        return x

    def _L0_ffn_ref(x, w1_w, w1_s, w2_w, w2_s, h1_w, h1_s, h2_w, h2_s, w3_w, w3_s):
        import jax, jax.numpy as jnp
        import numpy as np
        D_IN, D_HID = (128, 512)

        def _ternary(key, shape):
            return jax.random.randint(key, shape, -1, 2).astype(jnp.float32)

        def _tlin(x, w, s):
            return jnp.einsum('bsi,oi->bso', x, w) * s
        h = jax.nn.silu(_tlin(x, w1_w, w1_s)) * _tlin(x, w2_w, w2_s)
        h = jax.nn.gelu(_tlin(h, h1_w, h1_s), approximate=False)
        h = jax.nn.gelu(_tlin(h, h2_w, h2_s), approximate=False)
        return _tlin(h, w3_w, w3_s)
    x = L0_attn_x
    x = x + _layernorm(_L0_attn_ref(_layernorm(x, axis=-1), L0_attn_ln1_s, L0_attn_ln1_b, L0_attn_ln2_s, L0_attn_ln2_b, L0_attn_tmk, L0_attn_tmv, L0_attn_tmr, L0_attn_w_decay, L0_attn_u_first, L0_attn_Wk, L0_attn_Wv, L0_attn_Wr, L0_attn_Wo, L0_attn_f_tmk, L0_attn_f_tmr, L0_attn_fWk, L0_attn_fWr, L0_attn_fWv), axis=-1)
    x = x + _layernorm(_L0_ffn_ref(_layernorm(x, axis=-1), L0_ffn_w1_w, L0_ffn_w1_s, L0_ffn_w2_w, L0_ffn_w2_s, L0_ffn_h1_w, L0_ffn_h1_s, L0_ffn_h2_w, L0_ffn_h2_s, L0_ffn_w3_w, L0_ffn_w3_s), axis=-1)
    return x

_drawn_inputs = setup_inputs


def setup_inputs(seed=0):
    import zlib

    import numpy as np

    out = dict(_drawn_inputs(seed))
    spreads = {'L0_attn_ln1_s': (1.0, 0.2),
     'L0_attn_ln1_b': (0.0, 0.1),
     'L0_attn_ln2_s': (1.0, 0.2),
     'L0_attn_ln2_b': (0.0, 0.1)}
    factors = {}
    for name, (base, spread) in spreads.items():
        noise = np.random.default_rng([zlib.crc32(name.encode()), seed]).standard_normal(out[name].shape)
        drawn = base * np.exp(spread * noise) if base else spread * noise
        out[name] = jnp.asarray(drawn.astype(out[name].dtype))
    for name, factor in factors.items():
        out[name] = (out[name] * factor).astype(out[name].dtype)
    return out
```

```python
from contextlib import ExitStack

import concourse.bass as bass
from concourse import mybir

F32 = mybir.dt.float32
F32R = mybir.dt.float32r
BF16 = mybir.dt.bfloat16
I32 = mybir.dt.int32
ALU = mybir.AluOpType
ACT = mybir.ActivationFunctionType
AX_X = mybir.AxisListType.X
RMAX = bass.bass_isa.ReduceOp.max

P = 128
EPS = 1e-5
NO_MAXIMUM = -1e38

VECTORS = ["ln1_s", "ln1_b", "ln2_s", "ln2_b", "tmk", "tmv", "tmr", "w_decay", "u_first", "f_tmk", "f_tmr"]
VEC = {name: n for n, name in enumerate(VECTORS)}
MIX = {"Wk": 0, "Wv": 1, "Wr": 2, "Wo": 3, "fWr": 4, "fWk": 5, "fWv": 9}


class Group:

    def __init__(self, pair, step):
        self.n = 2 * pair + step
        self.par = step % 2
        self.turn = pair + step // 2


def wait(eng, sem, count):
    if not isinstance(count, int) or count > 0:
        eng.wait_ge(sem, count)


def build(nc, x_in, vec_in, scale_in, mix_in, ffn_in, w3s_in, out):
    B, T, C = x_in.shape
    NB = 2
    N = NB * T
    J = N // P
    GROUPS = B // NB
    MB = ffn_in.shape[1]
    HB = (MB - 0) // 11
    assert C == P and N == 512 and 3 * HB + 2 * HB * HB == MB and GROUPS % 2 == 0
    W1, W2, H1, H2, W3 = 0, HB, 2 * HB, 2 * HB + HB * HB, 2 * HB + 2 * HB * HB
    STAGE = HB * HB

    x_tiles = x_in.rearrange("(g b) (h p) c -> g p (b h) c", b=NB, p=P)
    out_tiles = out.rearrange("(g b) (h p) c -> g p (b h) c", b=NB, p=P)

    with ExitStack() as ctx:
        def sb(name, shape, dt=F32):
            return ctx.enter_context(nc.sbuf_tensor(name, shape, dt))

        def bank(name, dt=F32, shape=(P, 512)):
            return ctx.enter_context(nc.psum_tensor(name, list(shape), dt))

        def sem(name):
            return ctx.enter_context(nc.semaphore(name))

        vec = sb("vec", [P, len(VECTORS)])
        scale = sb("scale", [P, 4, HB])
        w3s = sb("w3s", [P, C])
        mix = sb("mix", [P, mix_in.shape[1], P])
        w_hi = sb("w_hi", [P, MB, P], F32R)
        w_lo = sb("w_lo", [P, MB, P], F32R)
        w_rest = sb("w_rest", [P, 8])
        w_rest1 = sb("w_rest1", [P, 1])
        w_rest_all = sb("w_rest_all", [P, 1])
        neg_decay = sb("neg_decay", [P, 1])
        pos_decay = sb("pos_decay", [P, 1])
        u_plus_w = sb("u_plus_w", [P, 1])
        decay_row = sb("decay_row", [P, T])
        half_row = sb("half_row", [P, T])
        minus_half = sb("minus_half", [P, J])
        minus_one = sb("minus_one", [P, J])
        eps_row = sb("eps_row", [P, J])
        ident = sb("ident", [P, P])
        ident16 = sb("ident16", [P, P], BF16)

        xa = sb("xa", [P, 2, J, C])
        x1 = sb("x1", [P, 2, J, C])
        n1 = sb("n1", [P, J, C])
        bn1 = sb("bn1", [P, J, 6])
        mv1 = sb("mv1", [P, J, 2])
        ln01 = sb("ln01", [P, 6, J])
        z1 = sb("z1", [P, NB, T + 1])
        d1 = sb("d1", [P, NB, T])
        mixed1 = sb("mixed1", [P, 3, NB, T])
        o = sb("o", [P, NB, T + 1])
        e = sb("e", [P, NB, T])
        above = sb("above", [P, 2, NB, T])
        below = sb("below", [P, 2, NB, T])
        tanh_r = sb("tanh_r", [P, NB, T])
        bv = sb("bv", [P, 2, NB, T])
        pq = sb("pq", [P, 2, NB, T + 1])
        nd = sb("nd", [P, 2, NB, T])
        y = sb("y", [P, NB, T])
        yr = sb("yr", [P, NB, T])
        h_in = [sb(f"h_in{k}", [P, NB, T]) for k in range(2)]
        volt = [sb(f"volt{k}", [P, NB, T]) for k in range(2)]
        spikes = [sb(f"spikes{k}", [P, NB, T], BF16) for k in range(2)]
        fired = [sb(f"fired{k}", [P, 1]) for k in range(2)]
        fired_all = [sb(f"fired_all{k}", [P, 1]) for k in range(2)]
        cell = sb("cell", [P, NB])
        cell_mask = sb("cell_mask", [P, NB])
        half_cell = sb("half_cell", [P, NB])
        x2 = sb("x2", [P, 2, J, C])
        n2 = sb("n2", [P, J, C])
        bn2 = sb("bn2", [P, J, 6])
        mv2 = sb("mv2", [P, J, 2])
        ln2 = sb("ln2", [P, 3, J])
        z2 = sb("z2", [P, NB, T + 1])
        d2 = sb("d2", [P, NB, T])
        mixed2 = sb("mixed2", [P, 2, NB, T])
        tanh_r2 = sb("tanh_r2", [P, NB, T])
        kk = sb("kk", [P, HB, N])
        xb = sb("xb", [P, 2, J, C])
        x3 = sb("x3", [P, J, C])
        bn3 = sb("bn3", [P, J, 6])
        mv3 = sb("mv3", [P, J, 2])
        ln3 = sb("ln3", [P, 3, J])
        n3 = sb("n3", [P, J, C])
        xres = sb("xres", [P, 2, J, C])
        bn4 = sb("bn4", [P, J, 6])
        mv4 = sb("mv4", [P, J, 2])
        ln4 = sb("ln4", [P, 3, J])
        n4 = sb("n4", [P, J, C])
        f0_hi = sb("f0_hi", [P, 1, N], F32R)
        f0_lo = sb("f0_lo", [P, 1, N], F32R)
        gate = sb("gate", [P, 2, N])
        hid = sb("hid", [P, HB, N])
        ac_hi = sb("ac_hi", [P, HB, N], F32R)
        ac_lo = sb("ac_lo", [P, HB, N], F32R)
        b_hi = sb("b_hi", [P, HB, N], F32R)
        b_lo = sb("b_lo", [P, HB, N], F32R)
        f_out = sb("f_out", [P, J, C])
        bn5 = sb("bn5", [P, J, 6])
        mv5 = sb("mv5", [P, J, 2])
        ln5 = sb("ln5", [P, 3, J])
        n5 = sb("n5", [P, J, C])
        y_out = sb("y_out", [P, J, C])

        p_turn = bank("p_turn")
        p_spk = bank("p_spk", BF16, (P, 2, 512))
        p_k = bank("p_k")
        p_v = bank("p_v")
        p_m = [bank(f"p_m{k}") for k in range(2)]
        p_f = [bank(f"p_f{k}") for k in range(2)]

        s_const = sem("s_const")
        s_stage = sem("s_stage")
        s_pool_const = sem("s_pool_const")
        s_ident0 = sem("s_ident0")
        s_pos = sem("s_pos")
        s_vec = sem("s_vec")
        s_hi_w = sem("s_hi_w")
        s_lo_w = sem("s_lo_w")
        s_rest = sem("s_rest")
        s_rest_all = sem("s_rest_all")
        s_xa = [sem(f"s_xa{k}") for k in range(2)]
        s_xb = [sem(f"s_xb{k}") for k in range(2)]
        s_bn = {n: sem(f"s_bn{n}") for n in (1, 2, 3, 4, 5)}
        s_mv = {n: sem(f"s_mv{n}") for n in (1, 2, 3, 4, 5)}
        s_x1 = sem("s_x1")
        s_n = {n: sem(f"s_n{n}") for n in (1, 2, 3, 4, 5)}
        s_turned = {n: sem(f"s_turned{n}") for n in (1, 2, 4)}
        s_z1 = sem("s_z1")
        s_d1 = sem("s_d1")
        s_mixed1 = sem("s_mixed1")
        s_k = sem("s_k")
        s_v = sem("s_v")
        s_r = sem("s_r")
        s_o = sem("s_o")
        s_e = sem("s_e")
        s_bounds = sem("s_bounds")
        s_tanh_r = sem("s_tanh_r")
        s_expA = sem("s_expA")
        s_expB = sem("s_expB")
        s_bv = sem("s_bv")
        s_pq = sem("s_pq")
        s_apq = sem("s_apq")
        s_den = sem("s_den")
        s_num = sem("s_num")
        s_ln = sem("s_ln")
        s_inv = sem("s_inv")
        s_yr = sem("s_yr")
        s_y = sem("s_y")
        s_wo = sem("s_wo")
        s_h_in = [sem(f"s_h_in{k}") for k in range(2)]
        s_volt = [sem(f"s_volt{k}") for k in range(2)]
        s_fired = [sem(f"s_fired{k}") for k in range(2)]
        s_spikes = [sem(f"s_spikes{k}") for k in range(2)]
        s_fired_all = [sem(f"s_fired_all{k}") for k in range(2)]
        s_spk_tok = [sem(f"s_spk_tok{k}") for k in range(2)]
        s_cell = sem("s_cell")
        s_x2 = sem("s_x2")
        s_z2 = sem("s_z2")
        s_d2 = sem("s_d2")
        s_mixed2 = sem("s_mixed2")
        s_r2 = sem("s_r2")
        s_tanh_r2 = sem("s_tanh_r2")
        s_fk = sem("s_fk")
        s_relu = sem("s_relu")
        s_square = sem("s_square")
        s_fv = sem("s_fv")
        s_x3 = sem("s_x3")
        s_xres = sem("s_xres")
        s_f0_hi = sem("s_f0_hi")
        s_f0_lo = sem("s_f0_lo")
        s_ab = sem("s_ab")
        s_gate = sem("s_gate")
        s_swiglu = sem("s_swiglu")
        s_h = {1: sem("s_h1"), 2: sem("s_h2")}
        s_gelu = {1: sem("s_gelu1"), 2: sem("s_gelu2")}
        s_hi = {n: sem(f"s_hi{n}") for n in (1, 2, 3)}
        s_lo = {n: sem(f"s_lo{n}") for n in (1, 2, 3)}
        s_w3 = sem("s_w3")
        s_f_out = sem("s_f_out")
        s_y_out = sem("s_y_out")
        s_stored = sem("s_stored")
        s_steps = {n: sem(f"s_steps{n}") for n in (1, 2, 3, 4, 5)}

        s_apart = sem("s_apart")

        def apart(eng):
            eng.sem_inc(s_apart, 1)

        def col(name):
            return vec[:, VEC[name]:VEC[name] + 1]

        def flat(t):
            return t.rearrange("p b t -> p (b t)")

        parts = [(W1, 2 * HB), (H1, HB * HB), (H2, HB * HB), (W3, HB)]
        block = ctx.enter_context(nc.Block())

        def schedule(fori, turn):
            def on(i):
                return {"shift_k": i + 1 < GROUPS, "wkv": 0 <= i < GROUPS, "channel": 0 <= i - 1 < GROUPS,
                        "ffn": 0 <= i - 2 < GROUPS}
            for i in range(-1, 4):
                turn(i // 2, i % 2, on(i))
            with fori(2, GROUPS // 2 - 1) as pair:
                turn(pair, 0, on(4))
                turn(pair, 1, on(5))
            for i in range(GROUPS - 2, GROUPS + 2):
                turn(i // 2, i % 2, on(i))

        @block.sync
        def _(sp):
            sp.dma_start(vec[:, :], vec_in).then_inc(s_const, 16)
            sp.dma_start(mix[:, :, :], mix_in).then_inc(s_const, 16)
            sp.dma_start(scale[:, :, :], scale_in).then_inc(s_const, 16)
            sp.dma_start(w3s[:, :], w3s_in.partition_broadcast(P)).then_inc(s_const, 16)

            def load_a(g):
                wait(sp, s_x1, g.n - 1)
                sp.dma_start(xa[:, g.par], x_tiles[g.n]).then_inc(s_xa[g.par], 16)

            def load_b(g):
                wait(sp, s_xres, g.n - 1)
                sp.dma_start(xb[:, g.par], x_tiles[g.n]).then_inc(s_xb[g.par], 16)

            load_a(Group(0, 0))
            for n, (first, count) in enumerate(parts):
                if n:
                    sp.wait_ge(s_hi_w, n)
                    sp.wait_ge(s_lo_w, n)
                stage = kk[:, :, :].rearrange("p h (b c) -> p (h b) c", c=P)
                sp.dma_start(stage[:, 0:count], ffn_in[:, first:first + count]).then_inc(s_stage, 16)

            def turn(pair, step, on):
                if on["shift_k"] and on.get("more", True):
                    pass
                g = Group(pair, step)
                if on["next"]:
                    load_a(Group(pair, step + 2))
                if on["wkv"]:
                    load_b(g)
                if on["ffn"]:
                    f = Group(pair, step - 2)
                    sp.wait_ge(s_y_out, f.n + 1)
                    sp.dma_start(out_tiles[f.n], y_out[:, :, :]).then_inc(s_stored, 16)

            def with_next(pair, step, on):
                i = 2 * pair + step
                on = dict(on, next=not isinstance(i, int) or i + 2 < GROUPS)
                turn(pair, step, on)

            schedule(sp.Fori, with_next)
            sp.wait_ge(s_stored, 16 * GROUPS)

        @block.gpsimd
        def _(pool):
            pool.memset(ident[:, :], 0.0).then_inc(s_ident0, 1)
            pool.memset(half_row[:, :], 0.5).then_inc(s_pool_const, 1)
            pool.memset(minus_half[:, :], -0.5).then_inc(s_pool_const, 1)
            pool.memset(minus_one[:, :], -1.0).then_inc(s_pool_const, 1)
            pool.memset(eps_row[:, :], EPS).then_inc(s_pool_const, 1)
            pool.memset(half_cell[:, :], 0.5).then_inc(s_pool_const, 1)
            pool.memset(z1[:, :, 0:1], 0.0).then_inc(s_pool_const, 1)
            pool.memset(z2[:, :, 0:1], 0.0).then_inc(s_pool_const, 1)
            pool.memset(o[:, :, 0:1], NO_MAXIMUM).then_inc(s_pool_const, 1)
            pool.memset(pq[:, :, :, 0:1], 0.0).then_inc(s_pool_const, 1)
            pool.wait_ge(s_ident0, 1)
            pool.affine_select(out=ident[:, :], in_=ident[:, :], compare_op=ALU.not_equal, fill=1.0, base=0,
                               pattern=[[-1, P]], channel_multiplier=1).then_inc(s_pool_const, 1)
            pool.wait_ge(s_rest, 1)
            pool.partition_all_reduce(w_rest_all[:, :], w_rest1[:, :], P, RMAX).then_inc(s_rest_all, 1)
            pool.wait_ge(s_pool_const, 10)

            def rstd(n, g, mv, work, steps=3):
                pool.wait_ge(s_mv[n], g.n + 1)
                pool.tensor_tensor(work[:, 2, :], mv[:, :, 1], eps_row[:, :], ALU.add).then_inc(s_steps[n], 1)
                pool.tensor_tensor(work[:, 1, :], mv[:, :, 0], minus_one[:, :], ALU.mult).then_inc(s_steps[n], 1)
                pool.wait_ge(s_steps[n], steps * g.n + 1)
                pool.tensor_tensor(work[:, 0, :], work[:, 2, :], minus_half[:, :], ALU.pow).then_inc(s_steps[n], 1)
                pool.wait_ge(s_steps[n], steps * g.n + 3)

            def center(out_, in_, work, j):
                return pool.tensor_scalar(out_, in_, work[:, 1, j:j + 1], work[:, 0, j:j + 1], ALU.add, ALU.mult)

            def norm_01(g):
                rstd(1, g, mv1, ln01, 7)
                pool.tensor_tensor(ln01[:, 3, :], ln01[:, 0, :], ln01[:, 0, :], ALU.mult).then_inc(s_steps[1], 1)
                pool.wait_ge(s_steps[1], 7 * g.n + 4)
                pool.tensor_tensor(ln01[:, 4, :], ln01[:, 3, :], mv1[:, :, 1], ALU.mult).then_inc(s_steps[1], 1)
                pool.wait_ge(s_steps[1], 7 * g.n + 5)
                pool.tensor_tensor(ln01[:, 5, :], ln01[:, 4, :], eps_row[:, :], ALU.add).then_inc(s_steps[1], 1)
                pool.wait_ge(s_steps[1], 7 * g.n + 6)
                pool.tensor_tensor(ln01[:, 3, :], ln01[:, 5, :], minus_half[:, :], ALU.pow).then_inc(s_steps[1], 1)
                wait(pool, s_x2, g.n - 1)
                apart(pool)
                for j in range(J):
                    last = center(x1[:, g.par, j], xa[:, g.par, j], ln01, j)
                last.then_inc(s_x1, 1)
                wait(pool, s_turned[1], g.n)
                pool.wait_ge(s_steps[1], 7 * (g.n + 1))
                pool.wait_ge(s_x1, g.n + 1)
                apart(pool)
                for j in range(J):
                    last = pool.tensor_scalar(n1[:, j], x1[:, g.par, j], ln01[:, 3, j:j + 1], 1.0, ALU.mult, ALU.mult)
                last.then_inc(s_n[1], 1)

            def shift_1(g):
                pool.wait_ge(s_z1, g.n + 1)
                wait(pool, s_mixed1, 3 * g.n)
                pool.tensor_tensor(d1[:, :, :], z1[:, :, 1:T + 1], z1[:, :, 0:T], ALU.subtract).then_inc(s_d1, 1)

            def norm_2(g):
                rstd(2, g, mv2, ln2)
                wait(pool, s_turned[2], g.n)
                apart(pool)
                for j in range(J):
                    last = center(n2[:, j], x2[:, g.par, j], ln2, j)
                last.then_inc(s_n[2], 1)

            def shift_2(g):
                pool.wait_ge(s_z2, g.n + 1)
                wait(pool, s_mixed2, 2 * g.n)
                pool.tensor_tensor(d2[:, :, :], z2[:, :, 1:T + 1], z2[:, :, 0:T], ALU.subtract).then_inc(s_d2, 1)

            def neurons(k, g):
                pool.wait_ge(s_fired[k], g.n + 1)
                pool.wait_ge(s_h_in[k], g.n + 1)
                apart(pool)
                pool.partition_all_reduce(fired_all[k][:, :], fired[k][:, :], P, RMAX).then_inc(s_fired_all[k], 1)
                pool.wait_ge(s_fired_all[k], g.n + 1)
                apart(pool)
                any_spike = pool.value_load(fired_all[k][0:1, 0:1].bitcast(I32))
                with pool.If(any_spike != 0):
                    pool.memset(cell[:, :], 0.0)
                    pool.drain()
                    with pool.Fori(0, T) as t:
                        pool.tensor_tensor(cell[:, :], cell[:, :], half_cell[:, :], ALU.mult)
                        pool.drain()
                        pool.tensor_tensor(cell[:, :], cell[:, :], h_in[k][:, :, bass.ds(t, 1)].rearrange("p b o -> p (b o)"), ALU.add)
                        pool.drain()
                        pool.tensor_scalar(cell_mask[:, :], cell[:, :], 1.0, None, ALU.is_ge)
                        pool.drain()
                        pool.tensor_copy(spikes[k][:, :, bass.ds(t, 1)].rearrange("p b o -> p (b o)"), cell_mask[:, :])
                        pool.tensor_scalar(cell_mask[:, :], cell_mask[:, :], -1.0, 1.0, ALU.mult, ALU.add)
                        pool.drain()
                        pool.tensor_tensor(cell[:, :], cell[:, :], cell_mask[:, :], ALU.mult)
                        pool.drain()
                pool.engine_nop().then_inc(s_spikes[k], 1)

            def norm_3(g):
                rstd(3, g, mv3, ln3)
                apart(pool)
                for j in range(J):
                    last = center(n3[:, j], x3[:, j], ln3, j)
                last.then_inc(s_n[3], 1)
                pool.wait_ge(s_xb[g.par], 16 * (g.turn + 1))
                wait(pool, s_y_out, g.n - 1)
                pool.wait_ge(s_n[3], g.n + 1)
                pool.tensor_tensor(xres[:, g.par], xb[:, g.par], n3[:, :, :], ALU.add).then_inc(s_xres, 1)

            def norm_4(g):
                rstd(4, g, mv4, ln4)
                wait(pool, s_turned[4], g.n)
                apart(pool)
                for j in range(J):
                    last = center(n4[:, j], xres[:, g.par, j], ln4, j)
                last.then_inc(s_n[4], 1)

            def norm_5(g):
                rstd(5, g, mv5, ln5)
                apart(pool)
                for j in range(J):
                    last = center(n5[:, j], f_out[:, j], ln5, j)
                last.then_inc(s_n[5], 1)
                wait(pool, s_stored, 16 * g.n)
                pool.wait_ge(s_n[5], g.n + 1)
                pool.tensor_tensor(y_out[:, :, :], n5[:, :, :], xres[:, g.par], ALU.add).then_inc(s_y_out, 1)

            def turn(pair, step, on):
                nxt, g, c, f = (Group(pair, step + k) for k in (1, 0, -1, -2))
                if on["channel"]:
                    neurons(1, c)
                if on["wkv"]:
                    neurons(0, g)
                if on["shift_k"]:
                    norm_01(nxt)
                if on["wkv"]:
                    norm_2(g)
                if on["channel"]:
                    norm_3(c)
                if on["shift_k"]:
                    shift_1(nxt)
                if on["wkv"]:
                    shift_2(g)
                if on["channel"]:
                    norm_4(c)
                if on["ffn"]:
                    norm_5(f)

            schedule(pool.Fori, turn)

        @block.scalar
        def _(act):
            act.wait_ge(s_const, 64)
            act.activation(pos_decay[:, :], col("w_decay"), ACT.Exp).then_inc(s_pos, 1)
            for n, (first, count) in enumerate(parts):
                stage = kk[:, :, :].rearrange("p h (b c) -> p (h b) c", c=P)
                act.wait_ge(s_stage, 16 * (n + 1))
                act.activation(w_hi[:, first:first + count], stage[:, 0:count], ACT.Copy).then_inc(s_hi_w, 1)
            act.wait_ge(s_vec, 1)

            def z_1(g):
                act.wait_ge(s_turned[1], g.n + 1)
                if isinstance(g.n, int) and g.n == 0:
                    act.wait_ge(s_pool_const, 10)
                wait(act, s_mixed1, 3 * g.n)
                act.activation(z1[:, :, 1:T + 1], p_turn[:, :].rearrange("p (b t) -> p b t", b=NB), ACT.Identity,
                               bias=col("ln1_b"), scale=col("ln1_s")).then_inc(s_z1, 1)

            def tanh_1(g):
                act.wait_ge(s_r, g.n + 1)
                wait(act, s_y, g.n)
                act.activation(flat(tanh_r[:, :, :]), p_m[0][:, :], ACT.Tanh, scale=0.5).then_inc(s_tanh_r, 1)

            def exps(g):
                act.preload_act_table_set("natural_log_exp_and_others")
                act.wait_ge(s_bounds, 4 * (g.n + 1))
                act.activation(above[:, :, :, :], above[:, :, :, :], ACT.Exp, scale=-1.0).then_inc(s_expA, 1)
                act.activation(below[:, :, :, :], below[:, :, :, :], ACT.Exp).then_inc(s_expB, 1)

            def inverse(g):
                act.wait_ge(s_den, g.n + 1)
                wait(act, s_yr, g.n)
                act.activation(y[:, :, :], nd[:, 1], ACT.Ln).then_inc(s_ln, 1)
                act.wait_ge(s_ln, g.n + 1)
                act.activation(y[:, :, :], y[:, :, :], ACT.Exp, scale=-1.0).then_inc(s_inv, 1)

            def neuron_input_1(g):
                act.wait_ge(s_wo, g.n + 1)
                wait(act, s_spikes[0], g.n)
                act.activation(flat(h_in[0][:, :, :]), p_k[:, :], ACT.Copy).then_inc(s_h_in[0], 1)

            def z_2(g):
                act.wait_ge(s_turned[2], g.n + 1)
                wait(act, s_mixed2, 2 * g.n)
                act.activation(z2[:, :, 1:T + 1], p_turn[:, :].rearrange("p (b t) -> p b t", b=NB), ACT.Identity,
                               bias=col("ln2_b"), scale=col("ln2_s")).then_inc(s_z2, 1)

            def tanh_2(g):
                act.wait_ge(s_r2, g.n + 1)
                wait(act, s_h_in[1], g.n)
                act.activation(flat(tanh_r2[:, :, :]), p_m[1][:, :], ACT.Tanh, scale=0.5).then_inc(s_tanh_r2, 1)

            def squares(g):
                for m in range(HB):
                    act.wait_ge(s_fk, HB * g.n + m + 1)
                    if m == 0:
                        wait(act, s_fv, g.n)
                        if isinstance(g.n, int) and g.n == 0:
                            act.wait_ge(s_lo_w, len(parts))
                    act.activation(kk[:, m], p_m[m % 2][:, :], ACT.Relu).then_inc(s_relu, 1)
                    act.wait_ge(s_relu, HB * g.n + m + 1)
                    act.activation(kk[:, m], kk[:, m], ACT.Square).then_inc(s_square, 1)

            def f0(g):
                act.wait_ge(s_turned[4], g.n + 1)
                wait(act, s_ab, 2 * HB * g.n)
                act.activation(f0_hi[:, 0], p_turn[:, :], ACT.Copy).then_inc(s_f0_hi, 1)

            def silu(g, m):
                act.wait_ge(s_ab, 2 * HB * g.n + 2 * m + 1)
                wait(act, s_swiglu, HB * g.n + max(m - 1, 0))
                act.activation(gate[:, m % 2], p_f[0][:, :], ACT.Silu, scale=scale[:, 0, m:m + 1]).then_inc(s_gate, 1)

            def high(layer, g, half):
                made = s_swiglu if layer == 1 else s_gelu[layer - 1]
                dst = b_hi if layer == 2 else ac_hi
                a, z = half * HB // 2, (half + 1) * HB // 2
                act.wait_ge(made, HB * g.n + z)
                if layer == 1:
                    wait(act, s_w3, g.n)
                elif layer == 2:
                    wait(act, s_h[2], HB * g.n)
                else:
                    act.wait_ge(s_h[1], HB * (g.n + 1))
                act.activation(dst[:, a:z], hid[:, a:z], ACT.Copy).then_inc(s_hi[layer], 1)

            def gelu(layer, g, m):
                act.wait_ge(s_h[layer], HB * g.n + m + 1)
                act.wait_ge(s_lo[layer], 2 * g.n + m // (HB // 2) + 1)
                act.activation(hid[:, m], p_f[m % 2][:, :], ACT.Gelu,
                               scale=scale[:, 1 + layer, m:m + 1]).then_inc(s_gelu[layer], 1)

            def turn(pair, step, on):
                nxt, g, c, f = (Group(pair, step + k) for k in (1, 0, -1, -2))
                if on["wkv"]:
                    exps(g)
                if on["channel"]:
                    squares(c)
                if on["wkv"]:
                    inverse(g)
                    neuron_input_1(g)
                if on["ffn"]:
                    silu(f, 0)
                    silu(f, 1)
                    silu(f, 2)
                    silu(f, 3)
                if on["shift_k"]:
                    z_1(nxt)
                if on["ffn"]:
                    high(1, f, 0)
                    high(1, f, 1)
                    gelu(1, f, 0)
                if on["wkv"]:
                    z_2(g)
                if on["ffn"]:
                    gelu(1, f, 1)
                    high(2, f, 0)
                    gelu(1, f, 2)
                if on["shift_k"]:
                    tanh_1(nxt)
                if on["ffn"]:
                    gelu(1, f, 3)
                    high(2, f, 1)
                if on["wkv"]:
                    tanh_2(g)
                if on["ffn"]:
                    gelu(2, f, 0)
                    gelu(2, f, 1)
                    high(3, f, 0)
                    gelu(2, f, 2)
                    gelu(2, f, 3)
                    high(3, f, 1)
                if on["channel"]:
                    f0(c)

            schedule(act.Fori, turn)

        @block.vector
        def _(dve):
            dve.wait_ge(s_pos, 1)
            dve.tensor_scalar(neg_decay[:, :], pos_decay[:, :], -1.0, None, ALU.mult).then_inc(s_vec, 1)
            dve.tensor_scalar(mix[:, MIX["Wo"]], mix[:, MIX["Wo"]], 0.25, None, ALU.mult).then_inc(s_vec, 1)
            dve.tensor_scalar(mix[:, MIX["fWv"]:MIX["fWv"] + HB], mix[:, MIX["fWv"]:MIX["fWv"] + HB], 0.25, None,
                              ALU.mult).then_inc(s_vec, 1)
            dve.wait_ge(s_vec, 1)
            dve.tensor_tensor(u_plus_w[:, :], col("u_first"), neg_decay[:, :], ALU.add).then_inc(s_vec, 1)
            dve.wait_ge(s_pool_const, 10)
            dve.tensor_scalar(decay_row[:, :], half_row[:, :], 0.0, neg_decay[:, 0:1], ALU.mult,
                              ALU.add).then_inc(s_vec, 1)
            dve.tensor_copy(ident16[:, :], ident[:, :]).then_inc(s_vec, 1)
            dve.wait_ge(s_vec, 6)
            for n, (first, count) in enumerate(parts):
                stage = kk[:, :, :].rearrange("p h (b c) -> p (h b) c", c=P)
                dve.wait_ge(s_hi_w, n + 1)
                hi, lo = w_hi[:, first:first + count], w_lo[:, first:first + count]
                dve.tensor_tensor(lo, stage[:, 0:count], hi.bitcast(F32), ALU.subtract).then_inc(s_lo_w, 1)
                dve.wait_ge(s_lo_w, n + 1)
                dve.tensor_reduce(w_rest[:, n:n + 1], lo.bitcast(F32), mybir.AxisListType.XY,
                                  ALU.max).then_inc(s_vec, 1)
                dve.tensor_reduce(w_rest[:, len(parts) + n:len(parts) + n + 1], lo.bitcast(F32),
                                  mybir.AxisListType.XY, ALU.min).then_inc(s_vec, 1)
            dve.wait_ge(s_vec, 6 + 2 * len(parts))
            dve.tensor_scalar(w_rest[:, len(parts):], w_rest[:, len(parts):], -1.0, None, ALU.mult).then_inc(s_vec, 1)
            dve.wait_ge(s_vec, 7 + 2 * len(parts))
            dve.tensor_reduce(w_rest1[:, :], w_rest[:, :], AX_X, ALU.max).then_inc(s_rest, 1)

            def statistics(n, g, bn, mv, tiles):
                for j in range(J):
                    last = dve.bn_stats(bn[:, j], tiles[:, j])
                last.then_inc(s_bn[n], 1)
                dve.wait_ge(s_bn[n], g.n + 1)
                apart(dve)
                for j in range(J):
                    last = dve.bn_aggr(mv[:, j], bn[:, j])
                last.then_inc(s_mv[n], 1)

            def stats_1(g):
                dve.wait_ge(s_xa[g.par], 16 * (g.turn + 1))
                wait(dve, s_n[1], g.n)
                statistics(1, g, bn1, mv1, xa[:, g.par])

            def mix_1(g):
                dve.wait_ge(s_d1, g.n + 1)
                wait(dve, s_r, g.n)
                for n, name in enumerate(("tmk", "tmv", "tmr")):
                    dve.scalar_tensor_tensor(mixed1[:, n], d1[:, :, :], col(name), z1[:, :, 0:T], ALU.mult,
                                             ALU.add).then_inc(s_mixed1, 1)

            def maximum(g):
                dve.wait_ge(s_k, g.n + 1)
                for b in range(NB):
                    last = dve.tensor_tensor_scan(o[:, b, 1:T + 1], decay_row[:, :], p_k[:, b * T:(b + 1) * T],
                                                  NO_MAXIMUM, ALU.add, ALU.max)
                last.then_inc(s_o, 1)
                dve.wait_ge(s_o, g.n + 1)
                dve.scalar_tensor_tensor(e[:, :, :], p_k[:, :].rearrange("p (b t) -> p b t", b=NB), col("u_first"),
                                         o[:, :, 0:T], ALU.add, ALU.subtract).then_inc(s_e, 1)

            def bounds(g):
                dve.wait_ge(s_e, g.n + 1)
                wait(dve, s_num, g.n)
                dve.tensor_scalar(above[:, 0], e[:, :, :], 0.0, None, ALU.max).then_inc(s_bounds, 1)
                dve.tensor_scalar(above[:, 1], e[:, :, :], u_plus_w[:, 0:1], 0.0, ALU.subtract,
                                  ALU.max).then_inc(s_bounds, 1)
                dve.tensor_scalar(below[:, 0], e[:, :, :], 0.0, None, ALU.min).then_inc(s_bounds, 1)
                dve.tensor_scalar(below[:, 1], e[:, :, :], u_plus_w[:, 0:1], 0.0, ALU.subtract,
                                  ALU.min).then_inc(s_bounds, 1)

            def sums(g):
                dve.wait_ge(s_expB, g.n + 1)
                dve.wait_ge(s_v, g.n + 1)
                for n in range(2):
                    last = dve.tensor_tensor(flat(bv[:, n]), flat(below[:, n]), p_v[:, :], ALU.mult)
                last.then_inc(s_bv, 1)
                for n in (1, 0):
                    new = below if n else bv
                    if n == 0:
                        dve.wait_ge(s_bv, g.n + 1)
                    for b in range(NB):
                        last = dve.tensor_tensor_scan(pq[:, n, b, 1:T + 1], above[:, 1, b], new[:, 1, b], 0.0,
                                                      ALU.mult, ALU.add)
                last.then_inc(s_pq, 1)
                dve.wait_ge(s_pq, g.n + 1)
                for n in (1, 0):
                    dve.tensor_tensor(nd[:, n], above[:, 0], pq[:, n, :, 0:T], ALU.mult).then_inc(s_apq, 1)
                dve.wait_ge(s_apq, 2 * g.n + 1)
                dve.tensor_tensor(nd[:, 1], nd[:, 1], below[:, 0], ALU.add).then_inc(s_den, 1)
                dve.wait_ge(s_apq, 2 * g.n + 2)
                dve.tensor_tensor(nd[:, 0], nd[:, 0], bv[:, 0], ALU.add).then_inc(s_num, 1)

            def ratio(g):
                dve.wait_ge(s_num, g.n + 1)
                dve.wait_ge(s_tanh_r, g.n + 1)
                wait(dve, s_wo, g.n)
                dve.scalar_tensor_tensor(nd[:, 0], tanh_r[:, :, :], 1.0, nd[:, 0], ALU.add, ALU.mult).then_inc(s_y, 1)
                dve.wait_ge(s_y, g.n + 1)
                dve.wait_ge(s_inv, g.n + 1)
                dve.tensor_tensor(yr[:, :, :], nd[:, 0], y[:, :, :], ALU.mult).then_inc(s_yr, 1)

            def fire(k, g, source):
                for b in range(NB):
                    last = dve.tensor_tensor_scan(volt[k][:, b], half_row[:, :], source[:, b * T:(b + 1) * T], 0.0,
                                                  ALU.mult, ALU.add)
                last.then_inc(s_volt[k], 1)
                dve.wait_ge(s_volt[k], g.n + 1)
                wait(dve, s_spk_tok[k], g.n)
                wait(dve, s_spikes[k], g.n)
                dve.tensor_scalar(spikes[k][:, :, :], volt[k][:, :, :], 1.0, None, ALU.is_ge, ALU.add,
                                  accum_out=fired[k][:, :]).then_inc(s_fired[k], 1)

            def fire_1(g):
                dve.wait_ge(s_h_in[0], g.n + 1)
                fire(0, g, flat(h_in[0][:, :, :]))

            def add_1(g):
                dve.wait_ge(s_spk_tok[0], g.n + 1)
                dve.wait_ge(s_x1, g.n + 1)
                wait(dve, s_x3, g.n - 1)
                wait(dve, s_n[2], g.n)
                dve.tensor_tensor(x2[:, g.par], p_spk[:, 0].rearrange("p (j c) -> p j c", c=C), x1[:, g.par],
                                  ALU.add).then_inc(s_x2, 1)
                dve.wait_ge(s_x2, g.n + 1)
                statistics(2, g, bn2, mv2, x2[:, g.par])

            def mix_2(g):
                dve.wait_ge(s_d2, g.n + 1)
                wait(dve, s_fk, HB * g.n)
                for n, name in enumerate(("f_tmr", "f_tmk")):
                    dve.scalar_tensor_tensor(mixed2[:, n], d2[:, :, :], col(name), z2[:, :, 0:T], ALU.mult,
                                             ALU.add).then_inc(s_mixed2, 1)

            def fire_2(g):
                dve.wait_ge(s_fv, g.n + 1)
                dve.wait_ge(s_tanh_r2, g.n + 1)
                wait(dve, s_spikes[1], g.n)
                dve.scalar_tensor_tensor(flat(h_in[1][:, :, :]), flat(tanh_r2[:, :, :]), 1.0, p_m[0][:, :], ALU.add,
                                         ALU.mult).then_inc(s_h_in[1], 1)
                dve.wait_ge(s_h_in[1], g.n + 1)
                fire(1, g, flat(h_in[1][:, :, :]))

            def add_2(g):
                dve.wait_ge(s_spk_tok[1], g.n + 1)
                wait(dve, s_n[3], g.n)
                dve.tensor_tensor(x3[:, :, :], p_spk[:, 1].rearrange("p (j c) -> p j c", c=C), x2[:, g.par],
                                  ALU.add).then_inc(s_x3, 1)
                dve.wait_ge(s_x3, g.n + 1)
                statistics(3, g, bn3, mv3, x3[:, :, :])

            def stats_4(g):
                dve.wait_ge(s_xres, g.n + 1)
                wait(dve, s_n[4], g.n)
                statistics(4, g, bn4, mv4, xres[:, g.par])

            def f0(g):
                dve.wait_ge(s_f0_hi, g.n + 1)
                dve.tensor_tensor(f0_lo[:, 0], p_turn[:, :], f0_hi[:, 0].bitcast(F32), ALU.subtract).then_inc(s_f0_lo, 1)

            def swiglu(g, m):
                dve.wait_ge(s_ab, 2 * HB * g.n + 2 * m + 2)
                dve.wait_ge(s_gate, HB * g.n + m + 1)
                if m == 0:
                    wait(dve, s_hi[3], 2 * g.n)
                dve.scalar_tensor_tensor(hid[:, m], p_f[1][:, :], scale[:, 1, m:m + 1], gate[:, m % 2], ALU.mult,
                                         ALU.mult).then_inc(s_swiglu, 1)

            def low(layer, g, half):
                hi, lo = (b_hi, b_lo) if layer == 2 else (ac_hi, ac_lo)
                a, z = half * HB // 2, (half + 1) * HB // 2
                dve.wait_ge(s_hi[layer], 2 * g.n + half + 1)
                dve.tensor_tensor(lo[:, a:z], hid[:, a:z], hi[:, a:z].bitcast(F32),
                                  ALU.subtract).then_inc(s_lo[layer], 1)

            def f_end(g):
                dve.wait_ge(s_w3, g.n + 1)
                wait(dve, s_n[5], g.n)
                dve.tensor_tensor(f_out[:, :, :], p_f[0][:, :].rearrange("p (j c) -> p j c", c=C),
                                  w3s[:, :].unsqueeze(1).to_broadcast([P, J, C]), ALU.mult).then_inc(s_f_out, 1)
                dve.wait_ge(s_f_out, g.n + 1)
                statistics(5, g, bn5, mv5, f_out[:, :, :])

            def turn(pair, step, on):
                nxt, g, c, f = (Group(pair, step + k) for k in (1, 0, -1, -2))
                if on["wkv"]:
                    sums(g)
                    ratio(g)
                if on["channel"]:
                    fire_2(c)
                if on["wkv"]:
                    fire_1(g)
                if on["ffn"]:
                    swiglu(f, 0)
                if on["shift_k"]:
                    stats_1(nxt)
                if on["ffn"]:
                    swiglu(f, 1)
                    swiglu(f, 2)
                    swiglu(f, 3)
                if on["channel"]:
                    add_2(c)
                if on["ffn"]:
                    low(1, f, 0)
                    low(1, f, 1)
                if on["wkv"]:
                    add_1(g)
                if on["shift_k"]:
                    mix_1(nxt)
                if on["ffn"]:
                    low(2, f, 0)
                if on["wkv"]:
                    mix_2(g)
                if on["shift_k"]:
                    maximum(nxt)
                if on["ffn"]:
                    low(2, f, 1)
                if on["shift_k"]:
                    bounds(nxt)
                if on["channel"]:
                    stats_4(c)
                if on["ffn"]:
                    low(3, f, 0)
                    low(3, f, 1)
                if on["channel"]:
                    f0(c)
                if on["ffn"]:
                    f_end(f)

            schedule(dve.Fori, turn)

        @block.tensor
        def _(pe):
            pe.wait_ge(s_const, 64)
            pe.wait_ge(s_vec, 6)
            pe.wait_ge(s_pool_const, 10)
            pe.wait_ge(s_hi_w, len(parts))
            pe.wait_ge(s_lo_w, len(parts))
            pe.wait_ge(s_rest_all, 1)
            long_weights = pe.value_load(w_rest_all[0:1, 0:1].bitcast(I32))

            def program(general):
                def turned(n, g, tiles):
                    for j in range(J):
                        last = pe.transpose(p_turn[:, j * P:(j + 1) * P], tiles[:, j], ident[:, :])
                    last.then_inc(s_turned[n], 1)

                def turn_1(g):
                    pe.wait_ge(s_n[1], g.n + 1)
                    wait(pe, s_f0_lo, g.n - 2)
                    turned(1, g, n1)

                def turn_2(g):
                    pe.wait_ge(s_n[2], g.n + 1)
                    if not isinstance(g.n, int) or g.n + 1 < GROUPS:
                        pe.wait_ge(s_z1, g.n + 2)
                    else:
                        pe.wait_ge(s_f0_lo, g.n - 1)
                    turned(2, g, n2)

                def turn_4(g):
                    pe.wait_ge(s_n[4], g.n + 1)
                    if not isinstance(g.n, int) or g.n + 1 < GROUPS:
                        pe.wait_ge(s_z2, g.n + 2)
                    else:
                        pe.wait_ge(s_f0_lo, g.n)
                    turned(4, g, n4)

                def time_product(g, n, name, bank_, done, freed, count):
                    pe.wait_ge(s_mixed1, 3 * g.n + n + 1)
                    for s in freed:
                        wait(pe, s, count)
                    pe.matmul(bank_[:, :], mix[:, MIX[name]], flat(mixed1[:, n]), start=True, stop=True).then_inc(done, 1)

                def kvr(g):
                    time_product(g, 0, "Wk", p_k, s_k, (s_h_in[0],), g.n)
                    time_product(g, 1, "Wv", p_v, s_v, (s_bv,), g.n)
                    time_product(g, 2, "Wr", p_m[0], s_r, (s_h_in[1],), g.n - 1)

                def out_product(g):
                    pe.wait_ge(s_yr, g.n + 1)
                    pe.wait_ge(s_e, g.n + 1)
                    pe.matmul(p_k[:, :], mix[:, MIX["Wo"]], flat(yr[:, :, :]), start=True, stop=True).then_inc(s_wo, 1)

                def spikes_turned(k, g):
                    pe.wait_ge(s_spikes[k], g.n + 1)
                    if k:
                        pe.wait_ge(s_x2, g.n + 1)
                    else:
                        wait(pe, s_x3, g.n)
                    tile = flat(spikes[k][:, :, :])
                    for j in range(J):
                        last = pe.transpose(p_spk[:, k, j * P:(j + 1) * P], tile[:, j * P:(j + 1) * P], ident16[:, :])
                    last.then_inc(s_spk_tok[k], 1)

                def r_product(g):
                    pe.wait_ge(s_mixed2, 2 * g.n + 1)
                    wait(pe, s_relu, HB * g.n)
                    pe.matmul(p_m[1][:, :], mix[:, MIX["fWr"]], flat(mixed2[:, 0]), start=True,
                              stop=True).then_inc(s_r2, 1)

                def channel_products(g):
                    pe.wait_ge(s_mixed2, 2 * g.n + 2)
                    for m in range(HB):
                        if m == 0:
                            if not isinstance(g.n, int) or g.n + 1 < GROUPS:
                                pe.wait_ge(s_tanh_r, g.n + 2)
                            else:
                                pe.wait_ge(s_h_in[1], g.n)
                        elif m == 1:
                            pe.wait_ge(s_tanh_r2, g.n + 1)
                        else:
                            pe.wait_ge(s_relu, HB * g.n + m - 1)
                        pe.matmul(p_m[m % 2][:, :], mix[:, MIX["fWk"] + m], flat(mixed2[:, 1]), start=True,
                                  stop=True).then_inc(s_fk, 1)
                    for m in range(HB):
                        if m == 0:
                            pe.wait_ge(s_relu, HB * g.n + HB - 1)
                        pe.wait_ge(s_square, HB * g.n + m + 1)
                        last = pe.matmul(p_m[0][:, :], mix[:, MIX["fWv"] + m], kk[:, m], start=(m == 0),
                                         stop=(m == HB - 1))
                    last.then_inc(s_fv, 1)

                def split_product(out_, blocks, hi, lo):
                    n = len(blocks)
                    for k, b in enumerate(blocks):
                        terms = [(w_hi, lo), (w_hi, hi)] + ([(w_lo, lo), (w_lo, hi)] if general else [])
                        for t, (w, x) in enumerate(terms):
                            last = pe.matmul(out_, w[:, b], x[:, k], start=(k == 0 and t == 0),
                                             stop=(k == n - 1 and t == len(terms) - 1))
                    return last

                def gate_products(g, m):
                    if m == 0:
                        pe.wait_ge(s_f0_hi, g.n + 1)
                        pe.wait_ge(s_f0_lo, g.n + 1)
                        wait(pe, s_f_out, g.n)
                    else:
                        pe.wait_ge(s_gate, HB * g.n + m)
                    split_product(p_f[0][:, :], [W1 + m], f0_hi, f0_lo).then_inc(s_ab, 1)
                    if m == 0:
                        wait(pe, s_gelu[2], HB * g.n)
                    else:
                        pe.wait_ge(s_swiglu, HB * g.n + m)
                    split_product(p_f[1][:, :], [W2 + m], f0_hi, f0_lo).then_inc(s_ab, 1)

                def hidden(layer, g, m):
                    if m >= 2:
                        pe.wait_ge(s_gelu[layer], HB * g.n + m - 1)
                    elif layer == 1:
                        pe.wait_ge(s_swiglu, HB * (g.n + 1))
                    else:
                        pe.wait_ge(s_gelu[1], HB * g.n + HB - 1 + m)
                    if m == 0:
                        pe.wait_ge(s_hi[layer], 2 * (g.n + 1))
                        pe.wait_ge(s_lo[layer], 2 * (g.n + 1))
                    hi, lo = (b_hi, b_lo) if layer == 2 else (ac_hi, ac_lo)
                    first = (H1 if layer == 1 else H2) + m * HB
                    split_product(p_f[m % 2][:, :], range(first, first + HB), hi, lo).then_inc(s_h[layer], 1)

                def out_tokens(g):
                    pe.wait_ge(s_hi[3], 2 * (g.n + 1))
                    pe.wait_ge(s_lo[3], 2 * (g.n + 1))
                    pe.wait_ge(s_gelu[2], HB * (g.n + 1))
                    for j in range(J):
                        tok = slice(j * P, (j + 1) * P)
                        for k in range(HB):
                            terms = [(ac_lo, w_hi), (ac_hi, w_hi)] + ([(ac_lo, w_lo), (ac_hi, w_lo)] if general else [])
                            for t, (x, w) in enumerate(terms):
                                last = pe.matmul(p_f[0][:, tok], x[:, k, tok], w[:, W3 + k],
                                                 start=(k == 0 and t == 0), stop=(k == HB - 1 and t == len(terms) - 1))
                    last.then_inc(s_w3, 1)

                def turn(pair, step, on):
                    nxt, g, c, f = (Group(pair, step + k) for k in (1, 0, -1, -2))
                    if on["channel"]:
                        channel_products(c)
                    if on["ffn"]:
                        gate_products(f, 0)
                    if on["wkv"]:
                        out_product(g)
                    if on["ffn"]:
                        gate_products(f, 1)
                    if on["channel"]:
                        spikes_turned(1, c)
                    if on["ffn"]:
                        gate_products(f, 2)
                        gate_products(f, 3)
                    if on["wkv"]:
                        spikes_turned(0, g)
                    if on["shift_k"]:
                        turn_1(nxt)
                    if on["ffn"]:
                        hidden(1, f, 0)
                    if on["wkv"]:
                        turn_2(g)
                    if on["ffn"]:
                        hidden(1, f, 1)
                    if on["shift_k"]:
                        kvr(nxt)
                    if on["ffn"]:
                        hidden(1, f, 2)
                    if on["wkv"]:
                        r_product(g)
                    if on["ffn"]:
                        hidden(1, f, 3)
                        for m in range(HB):
                            hidden(2, f, m)
                    if on["channel"]:
                        turn_4(c)
                    if on["ffn"]:
                        out_tokens(f)

                schedule(pe.Fori, turn)

            with pe.If(long_weights != 0):
                program(True)
            with pe.Else():
                program(False)


def kernel(**inputs):
    import numpy as np
    import concourse.bacc as bacc
    from concourse.bass_utils import run_bass_kernel_spmd

    a = {k[len("L0_attn_"):]: np.asarray(v) for k, v in inputs.items() if k.startswith("L0_attn_")}
    f = {k[len("L0_ffn_"):]: np.asarray(v) for k, v in inputs.items() if k.startswith("L0_ffn_")}
    hb = f["w1_w"].shape[0] // P

    def rows(w):
        return w.reshape(-1, P, w.shape[1]).transpose(1, 0, 2)

    def blocks(w):
        return w.reshape(w.shape[0] // P, P, w.shape[1] // P, P).transpose(3, 0, 2, 1).reshape(P, -1, P)

    arrays = {
        "x": a["x"],
        "vec": np.stack([a[n] for n in VECTORS], axis=1),
        "scale": np.stack([f[n].reshape(hb, P).T for n in ("w1_s", "w2_s", "h1_s", "h2_s")], axis=1),
        "mix": np.concatenate([a[n][:, None, :] for n in ("Wk", "Wv", "Wr", "Wo", "fWr")]
                              + [a["fWk"].reshape(P, hb, P), rows(a["fWv"])], axis=1),
        "ffn": np.concatenate([blocks(f[n]) for n in ("w1_w", "w2_w", "h1_w", "h2_w", "w3_w")], axis=1),
        "w3s": f["w3_s"],
    }
    arrays = {f"in_{k}": np.ascontiguousarray(v) for k, v in arrays.items()}
    nc = bacc.Bacc("TRN2", target_bir_lowering=False, num_devices=1)
    args = [nc.dram_tensor(k, v.shape, mybir.dt.from_np(v.dtype), kind="ExternalInput").ap() for k, v in arrays.items()]
    shape = arrays["in_x"].shape
    out = nc.dram_tensor("out", shape, F32, kind="ExternalOutput").ap()
    build(nc, *args, out)
    r = run_bass_kernel_spmd(nc, [arrays], core_ids=[0])
    return r.results[0]["out"]
```

```python
from contextlib import ExitStack

import concourse.bass as bass
from concourse import mybir

F32 = mybir.dt.float32
F32R = mybir.dt.float32r
BF16 = mybir.dt.bfloat16
I32 = mybir.dt.int32
ALU = mybir.AluOpType
ACT = mybir.ActivationFunctionType
AX_X = mybir.AxisListType.X
RMAX = bass.bass_isa.ReduceOp.max

P = 128
EPS = 1e-5
NO_MAXIMUM = -1e38

VECTORS = ["ln1_s", "ln1_b", "ln2_s", "ln2_b", "tmk", "tmv", "tmr", "w_decay", "u_first", "f_tmk", "f_tmr", "w3_s"]
VEC = {name: n for n, name in enumerate(VECTORS)}
MIX = {"Wk": 0, "Wv": 1, "Wr": 2, "Wo": 3, "fWr": 4, "fWk": 5, "fWv": 9}


POOL_BLOCKS = {1: (1,), 2: (1,), 3: (1, 2)}


class Group:

    def __init__(self, pair, step):
        self.n = 2 * pair + step
        self.par = step % 2
        self.turn = pair + step // 2


def wait(eng, sem, count):
    if not isinstance(count, int) or count > 0:
        eng.wait_ge(sem, count)


def build(nc, x_in, vec_in, scale_in, mix_in, ffn_in, out):
    B, T, C = x_in.shape
    NB = 2
    N = NB * T
    J = N // P
    GROUPS = B // NB
    MB = ffn_in.shape[1]
    HB = (MB - 0) // 11
    assert C == P and N == 512 and 3 * HB + 2 * HB * HB == MB and GROUPS % 2 == 0
    H1, H2, W1, W2, W3 = 0, HB * HB, 2 * HB * HB, 2 * HB * HB + HB, 2 * HB * HB + 2 * HB

    x_tiles = x_in.rearrange("(g b) (h p) c -> g p (b h) c", b=NB, p=P)
    out_tiles = out.rearrange("(g b) (h p) c -> g p (b h) c", b=NB, p=P)

    with ExitStack() as ctx:
        def sb(name, shape, dt=F32):
            return ctx.enter_context(nc.sbuf_tensor(name, shape, dt))

        def bank(name, dt=F32, shape=(P, 512)):
            return ctx.enter_context(nc.psum_tensor(name, list(shape), dt))

        def sem(name):
            return ctx.enter_context(nc.semaphore(name))

        vec = sb("vec", [P, len(VECTORS)])
        scale = sb("scale", [P, 4, HB])
        mix = sb("mix", [P, mix_in.shape[1], P])
        w_hi = sb("w_hi", [P, MB, P], F32R)
        w_lo = sb("w_lo", [P, MB, P], F32R)
        w_rest = sb("w_rest", [P, 3])
        w_rest1 = sb("w_rest1", [P, 1])
        w_rest_all = sb("w_rest_all", [P, 1])
        neg_decay = sb("neg_decay", [P, 1])
        pos_decay = sb("pos_decay", [P, 1])
        u_plus_w = sb("u_plus_w", [P, 1])
        decay_row = sb("decay_row", [P, T])
        half_row = sb("half_row", [P, T])
        minus_half = sb("minus_half", [P, 2, J])
        minus_one = sb("minus_one", [P, J])
        neg_mean = {n: sb(f"neg_mean{n}", [P, J]) for n in (1, 3, 5)}
        eps_row = sb("eps_row", [P, J])
        ident = sb("ident", [P, P])
        ident16 = sb("ident16", [P, P], BF16)

        xa = sb("xa", [P, 2, J, C])
        x1 = sb("x1", [P, 2, J, C])
        n1 = sb("n1", [P, J, C])
        bn1 = sb("bn1", [P, J, 6])
        mv1 = sb("mv1", [P, J, 2])
        var1 = sb("var1", [P, 2, J])
        rstd1 = sb("rstd1", [P, 2, J])
        z1 = sb("z1", [P, NB, T + 1])
        d1 = sb("d1", [P, NB, T])
        mixed1 = sb("mixed1", [P, 3, NB, T])
        o = sb("o", [P, NB, T + 1])
        e = sb("e", [P, NB, T])
        factors = sb("factors", [P, 4, NB, T])
        tanh_r = sb("tanh_r", [P, NB, T])
        bv = sb("bv", [P, 2, NB, T])
        pq = sb("pq", [P, 2, NB, T + 1])
        nd = sb("nd", [P, 2, NB, T])
        y = sb("y", [P, NB, T])
        yr = sb("yr", [P, NB, T])
        h_in = [sb(f"h_in{k}", [P, NB, T]) for k in range(2)]
        volt = [sb(f"volt{k}", [P, NB, T]) for k in range(2)]
        spikes = [sb(f"spikes{k}", [P, NB, T], BF16) for k in range(2)]
        fired = [sb(f"fired{k}", [P, 1]) for k in range(2)]
        fired_all = [sb(f"fired_all{k}", [P, 1]) for k in range(2)]
        cell = sb("cell", [P, NB])
        cell_mask = sb("cell_mask", [P, NB])
        half_cell = sb("half_cell", [P, NB])
        x2 = sb("x2", [P, 2, J, C])
        n2 = sb("n2", [P, J, C])
        bn2 = sb("bn2", [P, J, 6])
        mv2 = sb("mv2", [P, J, 2])
        var2 = sb("var2", [P, J])
        rstd2 = sb("rstd2", [P, J])
        z2 = sb("z2", [P, NB, T + 1])
        d2 = sb("d2", [P, NB, T])
        mixed2 = sb("mixed2", [P, 2, NB, T])
        tanh_r2 = sb("tanh_r2", [P, NB, T])
        kk = sb("kk", [P, HB, N])
        xb = sb("xb", [P, 2, J, C])
        x3 = sb("x3", [P, J, C])
        bn3 = sb("bn3", [P, J, 6])
        mv3 = sb("mv3", [P, J, 2])
        var3 = sb("var3", [P, J])
        rstd3 = sb("rstd3", [P, J])
        n3 = sb("n3", [P, J, C])
        xres = sb("xres", [P, 2, J, C])
        bn4 = sb("bn4", [P, J, 6])
        mv4 = sb("mv4", [P, J, 2])
        var4 = sb("var4", [P, J])
        rstd4 = sb("rstd4", [P, J])
        n4 = sb("n4", [P, J, C])
        f0_hi = sb("f0_hi", [P, 1, N], F32R)
        f0_lo = sb("f0_lo", [P, 1, N], F32R)
        gate = sb("gate", [P, 2, N])
        hid = sb("hid", [P, HB, N])
        ac_hi = sb("ac_hi", [P, HB, N], F32R)
        ac_lo = sb("ac_lo", [P, HB, N], F32R)
        b_hi = sb("b_hi", [P, HB, N], F32R)
        b_lo = sb("b_lo", [P, HB, N], F32R)
        f_cm = sb("f_cm", [P, N])
        f_out = sb("f_out", [P, J, C])
        bn5 = sb("bn5", [P, J, 6])
        mv5 = sb("mv5", [P, J, 2])
        var5 = sb("var5", [P, J])
        rstd5 = sb("rstd5", [P, J])
        y_out = sb("y_out", [P, J, C])

        p_turn = bank("p_turn")
        p_spk = bank("p_spk", BF16, (P, 2, 512))
        p_k = bank("p_k")
        p_v = bank("p_v")
        p_m = [bank(f"p_m{k}") for k in range(2)]
        p_f = [bank(f"p_f{k}") for k in range(2)]

        s_vec_in = sem("s_vec_in")
        s_mix_in = sem("s_mix_in")
        s_channel_in = sem("s_channel_in")
        s_stage = [sem(f"s_stage{k}") for k in range(2)]
        s_pool_const = sem("s_pool_const")
        s_ident0 = sem("s_ident0")
        s_pos = sem("s_pos")
        s_vec = sem("s_vec")
        s_hi_w = sem("s_hi_w")
        s_lo_w = sem("s_lo_w")
        s_rest = sem("s_rest")
        s_rest1 = sem("s_rest1")
        s_quarter = sem("s_quarter")
        s_rest_all = sem("s_rest_all")
        s_xa = [sem(f"s_xa{k}") for k in range(2)]
        s_xb = [sem(f"s_xb{k}") for k in range(2)]
        s_bn = {n: sem(f"s_bn{n}") for n in (1, 2, 3, 4, 5)}
        s_mv = {n: sem(f"s_mv{n}") for n in (1, 2, 3, 4, 5)}
        s_x1 = sem("s_x1")
        s_n = {n: sem(f"s_n{n}") for n in (1, 2, 3, 4, 5)}
        s_turned = {n: sem(f"s_turned{n}") for n in (1, 2, 4, 5)}
        s_z1 = sem("s_z1")
        s_d1 = sem("s_d1")
        s_mixed1 = sem("s_mixed1")
        s_k = sem("s_k")
        s_v = sem("s_v")
        s_r = sem("s_r")
        s_o = sem("s_o")
        s_e = sem("s_e")
        s_bounds = sem("s_bounds")
        s_under = sem("s_under")
        s_tanh_r = sem("s_tanh_r")
        s_expA = sem("s_expA")
        s_expB = sem("s_expB")
        s_bv = sem("s_bv")
        s_pq = sem("s_pq")
        s_apq = sem("s_apq")
        s_den = sem("s_den")
        s_num = sem("s_num")
        s_ln = sem("s_ln")
        s_inv = sem("s_inv")
        s_yr = sem("s_yr")
        s_y = sem("s_y")
        s_wo = sem("s_wo")
        s_h_in = [sem(f"s_h_in{k}") for k in range(2)]
        s_volt = [sem(f"s_volt{k}") for k in range(2)]
        s_fired = [sem(f"s_fired{k}") for k in range(2)]
        s_spikes = [sem(f"s_spikes{k}") for k in range(2)]
        s_fired_all = [sem(f"s_fired_all{k}") for k in range(2)]
        s_spk_tok = [sem(f"s_spk_tok{k}") for k in range(2)]
        s_cell = sem("s_cell")
        s_x2 = sem("s_x2")
        s_z2 = sem("s_z2")
        s_d2 = sem("s_d2")
        s_mixed2 = sem("s_mixed2")
        s_r2 = sem("s_r2")
        s_tanh_r2 = sem("s_tanh_r2")
        s_fk = sem("s_fk")
        s_relu = sem("s_relu")
        s_square = sem("s_square")
        s_fv = sem("s_fv")
        s_x3 = sem("s_x3")
        s_xres = sem("s_xres")
        s_f0_hi = sem("s_f0_hi")
        s_f0_lo = sem("s_f0_lo")
        s_ab = sem("s_ab")
        s_gate = sem("s_gate")
        s_swiglu = sem("s_swiglu")
        s_h = {1: sem("s_h1"), 2: sem("s_h2")}
        s_gelu = {1: sem("s_gelu1"), 2: sem("s_gelu2")}
        s_hi = {n: sem(f"s_hi{n}") for n in (1, 2, 3)}
        s_lo = {n: sem(f"s_lo{n}") for n in (1, 2, 3)}
        s_lo_pool = {n: sem(f"s_lo_pool{n}") for n in (1, 2, 3)}
        s_w3 = sem("s_w3")
        s_f_cm = sem("s_f_cm")
        s_f_out = sem("s_f_out")
        s_y_out = sem("s_y_out")
        s_stored = sem("s_stored")
        s_var = {n: sem(f"s_var{n}") for n in (1, 2, 3, 4, 5)}
        s_neg_mean = {n: sem(f"s_neg_mean{n}") for n in (1, 3, 5)}
        s_rstd = {n: sem(f"s_rstd{n}") for n in (1, 2, 3, 4, 5)}

        s_apart = sem("s_apart")

        def apart(eng):
            eng.sem_inc(s_apart, 1)

        def low_ready(eng, layer, g, m):
            others = [k for k in range(HB) if k not in POOL_BLOCKS[layer]]
            if m in POOL_BLOCKS[layer]:
                eng.wait_ge(s_lo_pool[layer], len(POOL_BLOCKS[layer]) * g.n + POOL_BLOCKS[layer].index(m) + 1)
            else:
                eng.wait_ge(s_lo[layer], len(others) * g.n + others.index(m) + 1)

        def split_low(eng, layer, g, m):
            hi, lo = (b_hi, b_lo) if layer == 2 else (ac_hi, ac_lo)
            eng.wait_ge(s_hi[layer], HB * g.n + m + 1)
            done = (s_lo_pool if m in POOL_BLOCKS[layer] else s_lo)[layer]
            eng.tensor_tensor(lo[:, m], hid[:, m], hi[:, m].bitcast(F32), ALU.subtract).then_inc(done, 1)

        def col(name):
            return vec[:, VEC[name]:VEC[name] + 1]

        def flat(t):
            return t.rearrange("p b t -> p (b t)")

        parts = [(kk, H1, HB * HB), (hid, H2, HB * HB), (hid, W1, 3 * HB)]

        def part(n):
            buffer, first, count = parts[n]
            staged = buffer[:, :, :].rearrange("p h (b c) -> p (h b) c", c=P)
            return staged[:, 0:count], slice(first, first + count)

        block = ctx.enter_context(nc.Block())

        def schedule(fori, turn, first=-1, last=GROUPS + 2):
            def on(i):
                return {"shift_k": i + 1 < GROUPS, "wkv": 0 <= i < GROUPS, "channel": 0 <= i - 1 < GROUPS,
                        "ffn": 0 <= i - 2 < GROUPS, "store": 0 <= i - 3 < GROUPS, "weights": i + 1 < len(parts)}
            loop = range(4, GROUPS - 2)
            for i in range(first, last + 1):
                if i == loop[0]:
                    with fori(loop[0] // 2, len(loop) // 2 + loop[0] // 2) as pair:
                        turn(pair, 0, on(4))
                        turn(pair, 1, on(5))
                elif i not in loop:
                    turn(i // 2, i % 2, on(i))

        @block.sync
        def _(sp):
            def load_a(g):
                wait(sp, s_x1, g.n - 1)
                wait(sp, s_n[1], g.n - 1)
                sp.dma_start(xa[:, g.par], x_tiles[g.n]).then_inc(s_xa[g.par], 16)

            def load_b(g):
                wait(sp, s_xres, g.n - 1)
                sp.dma_start(xb[:, g.par], x_tiles[g.n]).then_inc(s_xb[g.par], 16)

            def load_weights(n):
                staged, blocks = part(n)
                if n == 2:
                    sp.wait_ge(s_rest, n)
                sp.dma_start(staged, ffn_in[:, blocks]).then_inc(s_stage[min(n, 1)], 16)

            load_a(Group(0, 0))
            sp.dma_start(vec[:, :], vec_in).then_inc(s_vec_in, 16)
            split = MIX["fWk"]
            sp.dma_start(mix[:, 0:split], mix_in[:, 0:split]).then_inc(s_mix_in, 16)
            load_weights(0)
            sp.dma_start(mix[:, split:], mix_in[:, split:]).then_inc(s_channel_in, 16)
            sp.dma_start(scale[:, :, :], scale_in).then_inc(s_channel_in, 16)
            load_weights(1)
            load_a(Group(0, 1))
            load_b(Group(0, 0))
            load_weights(2)

            def turn(pair, step, on):
                g = Group(pair, step)
                if not isinstance(g.n, int) or 0 <= g.n < GROUPS - 2:
                    load_a(Group(pair, step + 2))
                if on["wkv"] and (not isinstance(g.n, int) or g.n > 0):
                    load_b(g)
                if on["store"]:
                    f = Group(pair, step - 3)
                    sp.wait_ge(s_y_out, f.n + 1)
                    sp.dma_start(out_tiles[f.n], y_out[:, :, :]).then_inc(s_stored, 16)

            schedule(sp.Fori, turn)
            sp.wait_ge(s_stored, 16 * GROUPS)

        @block.gpsimd
        def _(pool):
            pool.memset(ident[:, :], 0.0).then_inc(s_ident0, 1)
            pool.memset(half_row[:, :], 0.5).then_inc(s_pool_const, 1)
            pool.memset(minus_half[:, :, :], -0.5).then_inc(s_pool_const, 1)
            pool.memset(minus_one[:, :], -1.0).then_inc(s_pool_const, 1)
            pool.memset(eps_row[:, :], EPS).then_inc(s_pool_const, 1)
            pool.memset(half_cell[:, :], 0.5).then_inc(s_pool_const, 1)
            pool.memset(z1[:, :, 0:1], 0.0).then_inc(s_pool_const, 1)
            pool.memset(z2[:, :, 0:1], 0.0).then_inc(s_pool_const, 1)
            pool.memset(o[:, :, 0:1], NO_MAXIMUM).then_inc(s_pool_const, 1)
            pool.memset(pq[:, :, :, 0:1], 0.0).then_inc(s_pool_const, 1)
            pool.wait_ge(s_ident0, 1)
            pool.affine_select(out=ident[:, :], in_=ident[:, :], compare_op=ALU.not_equal, fill=1.0, base=0,
                               pattern=[[-1, P]], channel_multiplier=1).then_inc(s_pool_const, 1)
            pool.wait_ge(s_pool_const, 10)

            def rstd(n, g, mv, var, out_):
                pool.wait_ge(s_mv[n], g.n + 1)
                pool.tensor_tensor(var[:, :], mv[:, :, 1], eps_row[:, :], ALU.add).then_inc(s_var[n], 1)
                pool.wait_ge(s_var[n], g.n + 1)
                pool.tensor_tensor(out_[:, :], var[:, :], minus_half[:, 0], ALU.pow).then_inc(s_rstd[n], 1)

            def minus_mean(n, g, mv):
                pool.tensor_tensor(neg_mean[n][:, :], mv[:, :, 0], minus_one[:, :], ALU.mult).then_inc(s_neg_mean[n], 1)

            def centered(n, g, out_, in_, rstd):
                pool.wait_ge(s_neg_mean[n], g.n + 1)
                pool.wait_ge(s_rstd[n], g.n + 1)
                apart(pool)
                for j in range(J):
                    last = pool.tensor_scalar(out_[:, j], in_[:, j], neg_mean[n][:, j:j + 1], rstd[:, j:j + 1], ALU.add,
                                              ALU.mult)
                return last

            def rstd_1(g):
                pool.wait_ge(s_mv[1], g.n + 1)
                apart(pool)
                pool.tensor_scalar(var1[:, 0], mv1[:, :, 1], 1.0, EPS, ALU.mult, ALU.add).then_inc(s_var[1], 1)
                pool.tensor_scalar(var1[:, 1], mv1[:, :, 1], 1.0 + EPS, EPS * EPS, ALU.mult, ALU.add).then_inc(s_var[1], 1)
                minus_mean(1, g, mv1)
                pool.wait_ge(s_var[1], 2 * (g.n + 1))
                pool.tensor_tensor(rstd1[:, :, :], var1[:, :, :], minus_half[:, :, :], ALU.pow).then_inc(s_rstd[1], 1)

            def rstd_2(g):
                rstd(2, g, mv2, var2, rstd2)

            def rstd_3(g):
                rstd(3, g, mv3, var3, rstd3)
                minus_mean(3, g, mv3)

            def rstd_4(g):
                rstd(4, g, mv4, var4, rstd4)

            def rstd_5(g):
                rstd(5, g, mv5, var5, rstd5)
                minus_mean(5, g, mv5)

            def long_weights(i):
                if i + 2 == len(parts):
                    pool.wait_ge(s_rest1, 1)
                    pool.partition_all_reduce(w_rest_all[:, :], w_rest1[:, :], P, RMAX).then_inc(s_rest_all, 1)

            def weighted_sum(g, n):
                wait(pool, s_yr, g.n)
                pool.wait_ge(s_pq, 2 * (g.n + 1) - n)
                pool.tensor_tensor(nd[:, n], factors[:, 0], pq[:, n, :, 0:T], ALU.mult).then_inc(s_apq, 1)

            def shift_1(g):
                pool.wait_ge(s_z1, g.n + 1)
                wait(pool, s_mixed1, 3 * g.n)
                pool.tensor_tensor(d1[:, :, :], z1[:, :, 1:T + 1], z1[:, :, 0:T], ALU.subtract).then_inc(s_d1, 1)

            def shift_2(g):
                pool.wait_ge(s_z2, g.n + 1)
                wait(pool, s_mixed2, 2 * g.n)
                pool.tensor_tensor(d2[:, :, :], z2[:, :, 1:T + 1], z2[:, :, 0:T], ALU.subtract).then_inc(s_d2, 1)

            def neurons(k, g):
                pool.wait_ge(s_fired[k], g.n + 1)
                pool.wait_ge(s_h_in[k], g.n + 1)
                apart(pool)
                pool.partition_all_reduce(fired_all[k][:, :], fired[k][:, :], P, RMAX).then_inc(s_fired_all[k], 1)
                pool.wait_ge(s_fired_all[k], g.n + 1)
                apart(pool)
                any_spike = pool.value_load(fired_all[k][0:1, 0:1].bitcast(I32))
                with pool.If(any_spike != 0):
                    pool.memset(cell[:, :], 0.0)
                    pool.drain()
                    with pool.Fori(0, T) as t:
                        pool.tensor_tensor(cell[:, :], cell[:, :], half_cell[:, :], ALU.mult)
                        pool.drain()
                        pool.tensor_tensor(cell[:, :], cell[:, :], h_in[k][:, :, bass.ds(t, 1)].rearrange("p b o -> p (b o)"), ALU.add)
                        pool.drain()
                        pool.tensor_scalar(cell_mask[:, :], cell[:, :], 1.0, None, ALU.is_ge)
                        pool.drain()
                        pool.tensor_copy(spikes[k][:, :, bass.ds(t, 1)].rearrange("p b o -> p (b o)"), cell_mask[:, :])
                        pool.tensor_scalar(cell_mask[:, :], cell_mask[:, :], -1.0, 1.0, ALU.mult, ALU.add)
                        pool.drain()
                        pool.tensor_tensor(cell[:, :], cell[:, :], cell_mask[:, :], ALU.mult)
                        pool.drain()
                pool.engine_nop().then_inc(s_spikes[k], 1)

            def norm_0(g):
                wait(pool, s_x2, g.n - 1)
                centered(1, g, x1[:, g.par], xa[:, g.par], rstd1[:, 0]).then_inc(s_x1, 1)

            def norm_3(g):
                wait(pool, s_xres, g.n)
                centered(3, g, n3, x3, rstd3).then_inc(s_n[3], 1)

            def norm_5(g):
                centered(5, g, f_out, f_out, rstd5).then_inc(s_n[5], 1)

            def residual_3(g):
                pool.wait_ge(s_xb[g.par], 16 * (g.turn + 1))
                wait(pool, s_y_out, g.n - 1)
                pool.wait_ge(s_n[3], g.n + 1)
                pool.tensor_tensor(xres[:, g.par], xb[:, g.par], n3[:, :, :], ALU.add).then_inc(s_xres, 1)

            def residual_5(g):
                wait(pool, s_stored, 16 * g.n)
                pool.wait_ge(s_n[5], g.n + 1)
                pool.tensor_tensor(y_out[:, :, :], f_out[:, :, :], xres[:, g.par], ALU.add).then_inc(s_y_out, 1)

            def low(layer, g, m):
                split_low(pool, layer, g, m)

            def turn(pair, step, on):
                nxt, g, c, f, done = (Group(pair, step + k) for k in (1, 0, -1, -2, -3))
                if on["shift_k"]:
                    rstd_1(nxt)
                if on["wkv"]:
                    weighted_sum(g, 1)
                    weighted_sum(g, 0)
                if on["store"]:
                    rstd_5(done)
                if on["channel"]:
                    neurons(1, c)
                if on["shift_k"]:
                    shift_1(nxt)
                if on["ffn"]:
                    low(1, f, 1)
                if on["store"]:
                    norm_5(done)
                    residual_5(done)
                if on["wkv"]:
                    neurons(0, g)
                if on["channel"]:
                    rstd_3(c)
                if on["ffn"]:
                    low(2, f, 1)
                if on["channel"]:
                    norm_3(c)
                if on["weights"]:
                    long_weights(g.n)
                if on["wkv"]:
                    rstd_2(g)
                if on["channel"]:
                    residual_3(c)
                    rstd_4(c)
                if on["wkv"]:
                    shift_2(g)
                if on["ffn"]:
                    low(3, f, 1)
                    low(3, f, 2)
                if on["shift_k"]:
                    norm_0(nxt)

            schedule(pool.Fori, turn)

        @block.scalar
        def _(act):
            act.wait_ge(s_vec_in, 16)
            act.activation(pos_decay[:, :], col("w_decay"), ACT.Exp).then_inc(s_pos, 1)
            act.wait_ge(s_vec, 2)

            def high_weights(i):
                staged, blocks = part(i + 1)
                act.wait_ge(s_stage[min(i + 1, 1)], 16 * max(i + 1, 1))
                act.activation(w_hi[:, blocks], staged, ACT.Copy).then_inc(s_hi_w, 1)

            def z_1(g):
                act.wait_ge(s_turned[1], g.n + 1)
                if isinstance(g.n, int) and g.n == 0:
                    act.wait_ge(s_pool_const, 10)
                wait(act, s_mixed1, 3 * g.n)
                act.activation(z1[:, :, 1:T + 1], p_turn[:, :].rearrange("p (b t) -> p b t", b=NB), ACT.Identity,
                               bias=col("ln1_b"), scale=col("ln1_s")).then_inc(s_z1, 1)

            def tanh_1(g):
                act.wait_ge(s_r, g.n + 1)
                wait(act, s_y, g.n)
                act.activation(flat(tanh_r[:, :, :]), p_m[0][:, :], ACT.Tanh, scale=0.5).then_inc(s_tanh_r, 1)

            def under(g):
                act.wait_ge(s_e, g.n + 1)
                wait(act, s_num, g.n)
                act.activation(factors[:, 2], e[:, :, :], ACT.Relu, scale=-1.0).then_inc(s_under, 1)
                act.activation(factors[:, 3], e[:, :, :], ACT.Relu, scale=-1.0,
                               bias=u_plus_w[:, 0:1]).then_inc(s_under, 1)

            def exp_table(g):
                act.preload_act_table_set("natural_log_exp_and_others")

            def silu_table(g):
                act.preload_act_table_set("silu_and_others")

            def gelu_table(g):
                act.preload_act_table_set("gelu_and_others")

            def exps(g, n):
                if n == 0:
                    act.wait_ge(s_bounds, 2 * (g.n + 1))
                    act.activation(factors[:, 0:2], factors[:, 0:2], ACT.Exp, scale=-1.0).then_inc(s_expA, 1)
                else:
                    act.wait_ge(s_under, 2 * (g.n + 1))
                    act.activation(factors[:, 2:4], factors[:, 2:4], ACT.Exp, scale=-1.0).then_inc(s_expB, 1)

            def inverse(g):
                act.wait_ge(s_den, g.n + 1)
                wait(act, s_yr, g.n)
                act.activation(y[:, :, :], nd[:, 1], ACT.Ln).then_inc(s_ln, 1)
                act.wait_ge(s_ln, g.n + 1)
                act.activation(y[:, :, :], y[:, :, :], ACT.Exp, scale=-1.0).then_inc(s_inv, 1)

            def neuron_input_1(g):
                act.wait_ge(s_wo, g.n + 1)
                wait(act, s_spikes[0], g.n)
                act.activation(flat(h_in[0][:, :, :]), p_k[:, :], ACT.Copy).then_inc(s_h_in[0], 1)

            def z_2(g):
                act.wait_ge(s_turned[2], g.n + 1)
                wait(act, s_mixed2, 2 * g.n)
                act.activation(z2[:, :, 1:T + 1], p_turn[:, :].rearrange("p (b t) -> p b t", b=NB), ACT.Identity,
                               bias=col("ln2_b"), scale=col("ln2_s")).then_inc(s_z2, 1)

            def tanh_2(g):
                act.wait_ge(s_r2, g.n + 1)
                wait(act, s_h_in[1], g.n)
                act.activation(flat(tanh_r2[:, :, :]), p_m[1][:, :], ACT.Tanh, scale=0.5).then_inc(s_tanh_r2, 1)

            def relu(g, m):
                act.wait_ge(s_fk, HB * g.n + m + 1)
                wait(act, s_fv, g.n)
                if isinstance(g.n, int) and g.n == 0:
                    act.wait_ge(s_rest, 1)
                act.activation(kk[:, m], p_m[m % 2][:, :], ACT.Relu).then_inc(s_relu, 1)

            def square(g, m):
                act.wait_ge(s_relu, HB * g.n + m + 1)
                act.activation(kk[:, m], kk[:, m], ACT.Square).then_inc(s_square, 1)

            def f0(g):
                act.wait_ge(s_turned[4], g.n + 1)
                wait(act, s_ab, 2 * HB * g.n)
                act.activation(f0_hi[:, 0], p_turn[:, :], ACT.Copy).then_inc(s_f0_hi, 1)

            def silu(g, m):
                if isinstance(g.n, int) and g.n == 0:
                    act.wait_ge(s_channel_in, 32)
                act.wait_ge(s_ab, 2 * HB * g.n + 2 * m + 1)
                wait(act, s_swiglu, HB * g.n + max(m - 1, 0))
                act.activation(gate[:, m % 2], (p_v if m % 2 else p_f[0])[:, :], ACT.Silu, scale=scale[:, 0, m:m + 1]).then_inc(s_gate, 1)

            def high(layer, g, m):
                act.wait_ge(s_swiglu if layer == 1 else s_gelu[layer - 1], HB * g.n + m + 1)
                if layer == 1:
                    wait(act, s_w3, g.n)
                elif layer == 2:
                    wait(act, s_h[2], HB * g.n)
                else:
                    act.wait_ge(s_h[1], HB * (g.n + 1))
                dst = b_hi if layer == 2 else ac_hi
                act.activation(dst[:, m], hid[:, m], ACT.Copy).then_inc(s_hi[layer], 1)

            def gelu(layer, g, m):
                act.wait_ge(s_h[layer], HB * g.n + m + 1)
                low_ready(act, layer, g, m)
                act.activation(hid[:, m], p_f[m % 2][:, :], ACT.Gelu,
                               scale=scale[:, 1 + layer, m:m + 1]).then_inc(s_gelu[layer], 1)

            def output_scaled(g):
                act.wait_ge(s_w3, g.n + 1)
                wait(act, s_turned[5], g.n)
                act.activation(f_cm[:, :], p_f[0][:, :], ACT.Copy, scale=col("w3_s")).then_inc(s_f_cm, 1)

            def output_tokens(g):
                act.wait_ge(s_turned[5], g.n + 1)
                wait(act, s_y_out, g.n)
                act.activation(f_out[:, :, :], p_turn[:, :].rearrange("p (j c) -> p j c", c=C),
                               ACT.Copy).then_inc(s_f_out, 1)

            def turn(pair, step, on):
                nxt, g, c, f, done = (Group(pair, step + k) for k in (1, 0, -1, -2, -3))
                if on["wkv"]:
                    exp_table(g)
                    exps(g, 1)
                    exps(g, 0)
                if on["channel"]:
                    relu(c, 0)
                    relu(c, 1)
                if on["weights"]:
                    high_weights(g.n)
                if on["store"]:
                    output_scaled(done)
                if on["channel"]:
                    square(c, 0)
                    relu(c, 2)
                if on["store"]:
                    output_tokens(done)
                if on["channel"]:
                    square(c, 1)
                    square(c, 2)
                    relu(c, 3)
                    square(c, 3)
                if on["wkv"]:
                    inverse(g)
                if on["ffn"]:
                    silu_table(f)
                    silu(f, 0)
                    silu(f, 1)
                if on["shift_k"]:
                    z_1(nxt)
                if on["ffn"]:
                    high(1, f, 0)
                    silu(f, 2)
                    high(1, f, 1)
                    silu(f, 3)
                    high(1, f, 2)
                    high(1, f, 3)
                if on["wkv"]:
                    neuron_input_1(g)
                if on["ffn"]:
                    gelu_table(f)
                    gelu(1, f, 0)
                    high(2, f, 0)
                    gelu(1, f, 1)
                    high(2, f, 1)
                    gelu(1, f, 2)
                    high(2, f, 2)
                    gelu(1, f, 3)
                    high(2, f, 3)
                    gelu(2, f, 0)
                if on["shift_k"]:
                    under(nxt)
                if on["ffn"]:
                    gelu(2, f, 1)
                    high(3, f, 0)
                if on["wkv"]:
                    z_2(g)
                if on["ffn"]:
                    high(3, f, 1)
                    gelu(2, f, 2)
                if on["shift_k"]:
                    tanh_1(nxt)
                if on["ffn"]:
                    high(3, f, 2)
                    gelu(2, f, 3)
                if on["channel"]:
                    f0(c)
                if on["ffn"]:
                    high(3, f, 3)
                if on["wkv"]:
                    tanh_2(g)

            schedule(act.Fori, turn)

        @block.vector
        def _(dve):
            dve.wait_ge(s_pos, 1)
            dve.tensor_scalar(neg_decay[:, :], pos_decay[:, :], -1.0, None, ALU.mult).then_inc(s_vec, 1)
            dve.wait_ge(s_vec, 1)
            dve.tensor_tensor(u_plus_w[:, :], col("u_first"), neg_decay[:, :], ALU.add).then_inc(s_vec, 1)
            dve.wait_ge(s_pool_const, 10)
            dve.tensor_scalar(decay_row[:, :], half_row[:, :], 0.0, neg_decay[:, 0:1], ALU.mult,
                              ALU.add).then_inc(s_vec, 1)
            dve.tensor_copy(ident16[:, :], ident[:, :]).then_inc(s_vec, 1)
            dve.wait_ge(s_vec, 4)

            def scaled_weights(i):
                if i < 0:
                    first, count = MIX["Wo"], 1
                    dve.wait_ge(s_mix_in, 16)
                elif i == 0:
                    first, count = MIX["fWv"], HB
                    dve.wait_ge(s_channel_in, 32)
                else:
                    return
                dve.tensor_scalar(mix[:, first:first + count], mix[:, first:first + count], 0.25, None,
                                  ALU.mult).then_inc(s_quarter, 1)

            def low_weights(i):
                staged, blocks = part(i + 1)
                dve.wait_ge(s_hi_w, i + 2)
                dve.tensor_tensor(w_lo[:, blocks], staged, w_hi[:, blocks].bitcast(F32), ALU.subtract).then_inc(s_lo_w, 1)
                dve.wait_ge(s_lo_w, i + 2)
                dve.tensor_scalar(staged, w_lo[:, blocks].bitcast(F32), 0.0, None, ALU.not_equal, ALU.add,
                                  accum_out=w_rest[:, i + 1:i + 2]).then_inc(s_rest, 1)
                if i + 2 == len(parts):
                    dve.wait_ge(s_rest, len(parts))
                    dve.tensor_reduce(w_rest1[:, :], w_rest[:, :], AX_X, ALU.max).then_inc(s_rest1, 1)

            def statistics(n, g, bn, mv, tiles):
                for j in range(J):
                    last = dve.bn_stats(bn[:, j], tiles[:, j])
                last.then_inc(s_bn[n], 1)
                dve.wait_ge(s_bn[n], g.n + 1)
                apart(dve)
                for j in range(J):
                    last = dve.bn_aggr(mv[:, j], bn[:, j])
                last.then_inc(s_mv[n], 1)

            def stats_1(g):
                dve.wait_ge(s_xa[g.par], 16 * (g.turn + 1))
                wait(dve, s_n[1], g.n)
                wait(dve, s_x1, g.n)
                statistics(1, g, bn1, mv1, xa[:, g.par])

            def centered(n, g, out_, in_, mv, rstd):
                dve.wait_ge(s_rstd[n], g.n + 1)
                for j in range(J):
                    last = dve.tensor_scalar(out_[:, j], in_[:, j], mv[:, j, 0:1], rstd[:, j:j + 1], ALU.subtract,
                                             ALU.mult)
                return last

            def norm_1(g):
                wait(dve, s_turned[1], g.n)
                centered(1, g, n1, xa[:, g.par], mv1, rstd1[:, 1]).then_inc(s_n[1], 1)

            def norm_2(g):
                wait(dve, s_turned[2], g.n)
                centered(2, g, n2, x2[:, g.par], mv2, rstd2).then_inc(s_n[2], 1)

            def norm_4(g):
                wait(dve, s_turned[4], g.n)
                centered(4, g, n4, xres[:, g.par], mv4, rstd4).then_inc(s_n[4], 1)

            def mix_1(g):
                dve.wait_ge(s_d1, g.n + 1)
                wait(dve, s_r, g.n)
                for n, name in enumerate(("tmk", "tmv", "tmr")):
                    dve.scalar_tensor_tensor(mixed1[:, n], d1[:, :, :], col(name), z1[:, :, 0:T], ALU.mult,
                                             ALU.add).then_inc(s_mixed1, 1)

            def maximum(g):
                dve.wait_ge(s_k, g.n + 1)
                wait(dve, s_under, 2 * g.n)
                for b in range(NB):
                    last = dve.tensor_tensor_scan(o[:, b, 1:T + 1], decay_row[:, :], p_k[:, b * T:(b + 1) * T],
                                                  NO_MAXIMUM, ALU.add, ALU.max)
                last.then_inc(s_o, 1)
                dve.wait_ge(s_o, g.n + 1)
                dve.scalar_tensor_tensor(e[:, :, :], p_k[:, :].rearrange("p (b t) -> p b t", b=NB), col("u_first"),
                                         o[:, :, 0:T], ALU.add, ALU.subtract).then_inc(s_e, 1)

            def bounds(g):
                dve.wait_ge(s_e, g.n + 1)
                wait(dve, s_num, g.n)
                dve.tensor_scalar(factors[:, 0], e[:, :, :], 0.0, None, ALU.max).then_inc(s_bounds, 1)
                dve.tensor_scalar(factors[:, 1], e[:, :, :], u_plus_w[:, 0:1], 0.0, ALU.subtract,
                                  ALU.max).then_inc(s_bounds, 1)

            def sums(g):
                dve.wait_ge(s_expA, g.n + 1)
                dve.wait_ge(s_expB, g.n + 1)
                dve.wait_ge(s_v, g.n + 1)
                for n in range(2):
                    last = dve.tensor_tensor(flat(bv[:, n]), flat(factors[:, 2 + n]), p_v[:, :], ALU.mult)
                last.then_inc(s_bv, 1)
                wait(dve, s_apq, 2 * g.n)
                for n in (1, 0):
                    new = factors[:, 3] if n else bv[:, 1]
                    if n == 0:
                        dve.wait_ge(s_bv, g.n + 1)
                    for b in range(NB):
                        last = dve.tensor_tensor_scan(pq[:, n, b, 1:T + 1], factors[:, 1, b], new[:, b], 0.0,
                                                      ALU.mult, ALU.add)
                    last.then_inc(s_pq, 1)

            def fraction(g):
                dve.wait_ge(s_apq, 2 * g.n + 1)
                dve.tensor_tensor(nd[:, 1], nd[:, 1], factors[:, 2], ALU.add).then_inc(s_den, 1)
                dve.wait_ge(s_apq, 2 * g.n + 2)
                dve.tensor_tensor(nd[:, 0], nd[:, 0], bv[:, 0], ALU.add).then_inc(s_num, 1)

            def ratio(g):
                dve.wait_ge(s_num, g.n + 1)
                dve.wait_ge(s_tanh_r, g.n + 1)
                wait(dve, s_wo, g.n)
                dve.scalar_tensor_tensor(nd[:, 0], tanh_r[:, :, :], 1.0, nd[:, 0], ALU.add, ALU.mult).then_inc(s_y, 1)

            def ratio_end(g):
                dve.wait_ge(s_y, g.n + 1)
                dve.wait_ge(s_inv, g.n + 1)
                dve.tensor_tensor(yr[:, :, :], nd[:, 0], y[:, :, :], ALU.mult).then_inc(s_yr, 1)

            def fire(k, g, source):
                for b in range(NB):
                    last = dve.tensor_tensor_scan(volt[k][:, b], half_row[:, :], source[:, b * T:(b + 1) * T], 0.0,
                                                  ALU.mult, ALU.add)
                last.then_inc(s_volt[k], 1)
                dve.wait_ge(s_volt[k], g.n + 1)
                wait(dve, s_spk_tok[k], g.n)
                wait(dve, s_spikes[k], g.n)
                dve.tensor_scalar(spikes[k][:, :, :], volt[k][:, :, :], 1.0, None, ALU.is_ge, ALU.add,
                                  accum_out=fired[k][:, :]).then_inc(s_fired[k], 1)

            def fire_1(g):
                dve.wait_ge(s_h_in[0], g.n + 1)
                fire(0, g, flat(h_in[0][:, :, :]))

            def add_1(g):
                dve.wait_ge(s_spk_tok[0], g.n + 1)
                dve.wait_ge(s_x1, g.n + 1)
                wait(dve, s_x3, g.n - 1)
                wait(dve, s_n[2], g.n)
                dve.tensor_tensor(x2[:, g.par], p_spk[:, 0].rearrange("p (j c) -> p j c", c=C), x1[:, g.par],
                                  ALU.add).then_inc(s_x2, 1)
                dve.wait_ge(s_x2, g.n + 1)
                statistics(2, g, bn2, mv2, x2[:, g.par])

            def mix_2(g):
                dve.wait_ge(s_d2, g.n + 1)
                wait(dve, s_fk, HB * g.n)
                for n, name in enumerate(("f_tmr", "f_tmk")):
                    dve.scalar_tensor_tensor(mixed2[:, n], d2[:, :, :], col(name), z2[:, :, 0:T], ALU.mult,
                                             ALU.add).then_inc(s_mixed2, 1)

            def fire_2(g):
                dve.wait_ge(s_fv, g.n + 1)
                dve.wait_ge(s_tanh_r2, g.n + 1)
                wait(dve, s_spikes[1], g.n)
                dve.scalar_tensor_tensor(flat(h_in[1][:, :, :]), flat(tanh_r2[:, :, :]), 1.0, p_m[0][:, :], ALU.add,
                                         ALU.mult).then_inc(s_h_in[1], 1)
                dve.wait_ge(s_h_in[1], g.n + 1)
                fire(1, g, flat(h_in[1][:, :, :]))

            def add_2(g):
                dve.wait_ge(s_spk_tok[1], g.n + 1)
                wait(dve, s_n[3], g.n)
                dve.tensor_tensor(x3[:, :, :], p_spk[:, 1].rearrange("p (j c) -> p j c", c=C), x2[:, g.par],
                                  ALU.add).then_inc(s_x3, 1)
                dve.wait_ge(s_x3, g.n + 1)
                statistics(3, g, bn3, mv3, x3[:, :, :])

            def stats_4(g):
                dve.wait_ge(s_xres, g.n + 1)
                wait(dve, s_n[4], g.n)
                statistics(4, g, bn4, mv4, xres[:, g.par])

            def f0(g):
                dve.wait_ge(s_f0_hi, g.n + 1)
                dve.tensor_tensor(f0_lo[:, 0], p_turn[:, :], f0_hi[:, 0].bitcast(F32), ALU.subtract).then_inc(s_f0_lo, 1)

            def swiglu(g, m):
                dve.wait_ge(s_ab, 2 * HB * g.n + 2 * m + 2)
                dve.wait_ge(s_gate, HB * g.n + m + 1)
                wait(dve, s_lo[3], (HB - len(POOL_BLOCKS[3])) * g.n)
                wait(dve, s_lo_pool[3], len(POOL_BLOCKS[3]) * g.n)
                if isinstance(g.n, int) and g.n == 0:
                    dve.wait_ge(s_rest, len(parts))
                dve.scalar_tensor_tensor(hid[:, m], (p_m[1] if m % 2 else p_f[1])[:, :], scale[:, 1, m:m + 1], gate[:, m % 2], ALU.mult,
                                         ALU.mult).then_inc(s_swiglu, 1)

            def low(layer, g, m):
                split_low(dve, layer, g, m)

            def stats_5(g):
                dve.wait_ge(s_f_out, g.n + 1)
                wait(dve, s_n[5], g.n)
                statistics(5, g, bn5, mv5, f_out[:, :, :])

            def turn(pair, step, on):
                nxt, g, c, f, done = (Group(pair, step + k) for k in (1, 0, -1, -2, -3))
                if on["shift_k"]:
                    stats_1(nxt)
                if on["weights"]:
                    scaled_weights(g.n)
                if on["wkv"]:
                    sums(g)
                if on["shift_k"]:
                    norm_1(nxt)
                if on["store"]:
                    stats_5(done)
                if on["wkv"]:
                    fraction(g)
                    ratio(g)
                if on["channel"]:
                    fire_2(c)
                if on["ffn"]:
                    swiglu(f, 0)
                    swiglu(f, 1)
                if on["wkv"]:
                    ratio_end(g)
                if on["ffn"]:
                    low(1, f, 0)
                if on["weights"]:
                    low_weights(g.n)
                if on["ffn"]:
                    swiglu(f, 2)
                    swiglu(f, 3)
                    low(1, f, 2)
                    low(1, f, 3)
                if on["wkv"]:
                    fire_1(g)
                if on["channel"]:
                    add_2(c)
                if on["shift_k"]:
                    mix_1(nxt)
                if on["wkv"]:
                    add_1(g)
                if on["ffn"]:
                    low(2, f, 0)
                    low(2, f, 2)
                    low(2, f, 3)
                if on["shift_k"]:
                    maximum(nxt)
                if on["wkv"]:
                    norm_2(g)
                if on["channel"]:
                    stats_4(c)
                if on["shift_k"]:
                    bounds(nxt)
                if on["ffn"]:
                    low(3, f, 0)
                if on["channel"]:
                    norm_4(c)
                if on["wkv"]:
                    mix_2(g)
                if on["ffn"]:
                    low(3, f, 3)
                if on["channel"]:
                    f0(c)

            schedule(dve.Fori, turn)

        @block.tensor
        def _(pe):
            pe.wait_ge(s_pool_const, 10)
            pe.wait_ge(s_vec, 4)

            def program(general, **turns):
                def turned(n, g, tiles):
                    for j in range(J):
                        last = pe.transpose(p_turn[:, j * P:(j + 1) * P], tiles[:, j], ident[:, :])
                    last.then_inc(s_turned[n], 1)

                def turn_1(g):
                    pe.wait_ge(s_n[1], g.n + 1)
                    wait(pe, s_f0_lo, g.n - 2)
                    wait(pe, s_f_out, g.n - 3)
                    turned(1, g, n1)

                def turn_2(g):
                    pe.wait_ge(s_n[2], g.n + 1)
                    if not isinstance(g.n, int) or g.n + 1 < GROUPS:
                        pe.wait_ge(s_z1, g.n + 2)
                    else:
                        pe.wait_ge(s_f_out, g.n - 2)
                    turned(2, g, n2)

                def turn_4(g):
                    pe.wait_ge(s_n[4], g.n + 1)
                    if not isinstance(g.n, int) or g.n + 1 < GROUPS:
                        pe.wait_ge(s_z2, g.n + 2)
                    else:
                        pe.wait_ge(s_f_out, g.n - 1)
                    turned(4, g, n4)

                def time_product(g, n, name, bank_, done, freed, count):
                    pe.wait_ge(s_mixed1, 3 * g.n + n + 1)
                    if isinstance(g.n, int) and g.n == 0:
                        pe.wait_ge(s_mix_in, 16)
                    for s in freed:
                        wait(pe, s, count)
                    pe.matmul(bank_[:, :], mix[:, MIX[name]], flat(mixed1[:, n]), start=True, stop=True).then_inc(done, 1)

                def k_product(g):
                    time_product(g, 0, "Wk", p_k, s_k, (s_h_in[0],), g.n)

                def v_r_products(g):
                    wait(pe, s_gate, HB * (g.n - 2))
                    time_product(g, 1, "Wv", p_v, s_v, (s_bv,), g.n)
                    time_product(g, 2, "Wr", p_m[0], s_r, (s_h_in[1],), g.n - 1)

                def out_product(g):
                    pe.wait_ge(s_yr, g.n + 1)
                    pe.wait_ge(s_e, g.n + 1)
                    if isinstance(g.n, int) and g.n == 0:
                        pe.wait_ge(s_quarter, 1)
                    pe.matmul(p_k[:, :], mix[:, MIX["Wo"]], flat(yr[:, :, :]), start=True, stop=True).then_inc(s_wo, 1)

                def spikes_turned(k, g):
                    pe.wait_ge(s_spikes[k], g.n + 1)
                    if k:
                        pe.wait_ge(s_x2, g.n + 1)
                    else:
                        wait(pe, s_x3, g.n)
                    tile = flat(spikes[k][:, :, :])
                    for j in range(J):
                        last = pe.transpose(p_spk[:, k, j * P:(j + 1) * P], tile[:, j * P:(j + 1) * P], ident16[:, :])
                    last.then_inc(s_spk_tok[k], 1)

                def r_product(g):
                    pe.wait_ge(s_mixed2, 2 * g.n + 1)
                    wait(pe, s_relu, HB * g.n)
                    wait(pe, s_swiglu, HB * (g.n - 1))
                    pe.matmul(p_m[1][:, :], mix[:, MIX["fWr"]], flat(mixed2[:, 0]), start=True,
                              stop=True).then_inc(s_r2, 1)

                def channel_k(g, m):
                    if isinstance(g.n, int) and g.n == 0:
                        pe.wait_ge(s_channel_in, 32)
                    pe.wait_ge(s_mixed2, 2 * g.n + 2)
                    if m == 0:
                        if not isinstance(g.n, int) or g.n + 1 < GROUPS:
                            pe.wait_ge(s_tanh_r, g.n + 2)
                        else:
                            pe.wait_ge(s_h_in[1], g.n)
                    elif m == 1:
                        pe.wait_ge(s_tanh_r2, g.n + 1)
                    else:
                        pe.wait_ge(s_relu, HB * g.n + m - 1)
                    pe.matmul(p_m[m % 2][:, :], mix[:, MIX["fWk"] + m], flat(mixed2[:, 1]), start=True,
                              stop=True).then_inc(s_fk, 1)

                def channel_v(g):
                    if isinstance(g.n, int) and g.n == 0:
                        pe.wait_ge(s_quarter, 2)
                    for m in range(HB):
                        if m == 0:
                            pe.wait_ge(s_relu, HB * g.n + HB - 1)
                        pe.wait_ge(s_square, HB * g.n + m + 1)
                        last = pe.matmul(p_m[0][:, :], mix[:, MIX["fWv"] + m], kk[:, m], start=(m == 0),
                                         stop=(m == HB - 1))
                    last.then_inc(s_fv, 1)

                def split_product(out_, blocks, hi, lo, layer=None, g=None):
                    n = len(blocks)
                    for k, b in enumerate(blocks):
                        if layer:
                            pe.wait_ge(s_hi[layer], HB * g.n + k + 1)
                            low_ready(pe, layer, g, k)
                        terms = [(w_hi, lo), (w_hi, hi)] + ([(w_lo, lo), (w_lo, hi)] if general else [])
                        for t, (w, x) in enumerate(terms):
                            last = pe.matmul(out_, w[:, b], x[:, k], start=(k == 0 and t == 0),
                                             stop=(k == n - 1 and t == len(terms) - 1))
                    return last

                def gate_products(g, m):
                    if m == 0:
                        pe.wait_ge(s_f0_hi, g.n + 1)
                        pe.wait_ge(s_f0_lo, g.n + 1)
                        wait(pe, s_f_cm, g.n)
                        wait(pe, s_gelu[2], HB * g.n)
                    elif m == 1:
                        if not isinstance(g.n, int) or g.n + 2 < GROUPS:
                            pe.wait_ge(s_bv, g.n + 3)
                        if not isinstance(g.n, int) or g.n + 1 < GROUPS:
                            pe.wait_ge(s_relu, HB * (g.n + 2))
                        wait(pe, s_gate, HB * g.n)
                        wait(pe, s_swiglu, HB * g.n)
                    else:
                        pe.wait_ge(s_gate, HB * g.n + m - 1)
                        pe.wait_ge(s_swiglu, HB * g.n + m - 1)
                    to_gate, to_value = (p_v, p_m[1]) if m % 2 else p_f
                    split_product(to_gate[:, :], [W1 + m], f0_hi, f0_lo).then_inc(s_ab, 1)
                    split_product(to_value[:, :], [W2 + m], f0_hi, f0_lo).then_inc(s_ab, 1)

                def hidden(layer, g, m):
                    if m >= 2:
                        pe.wait_ge(s_gelu[layer], HB * g.n + m - 1)
                    elif layer == 1:
                        pe.wait_ge(s_swiglu, HB * g.n + 3)
                    else:
                        pe.wait_ge(s_gelu[1], HB * g.n + HB - 1 + m)
                    hi, lo = (b_hi, b_lo) if layer == 2 else (ac_hi, ac_lo)
                    first = (H1 if layer == 1 else H2) + m * HB
                    split_product(p_f[m % 2][:, :], range(first, first + HB), hi, lo,
                                  layer if m == 0 else None, g).then_inc(s_h[layer], 1)

                def last_product(g):
                    pe.wait_ge(s_gelu[2], HB * g.n + HB - 1)
                    split_product(p_f[0][:, :], range(W3, W3 + HB), ac_hi, ac_lo, 3, g).then_inc(s_w3, 1)

                def turn_5(g):
                    pe.wait_ge(s_f_cm, g.n + 1)
                    if not isinstance(g.n, int) or g.n + 1 < GROUPS:
                        pe.wait_ge(s_f0_lo, g.n + 2)
                    wait(pe, s_f_out, g.n)
                    for j in range(J):
                        last = pe.transpose(p_turn[:, j * P:(j + 1) * P], f_cm[:, j * P:(j + 1) * P], ident[:, :])
                    last.then_inc(s_turned[5], 1)

                def turn(pair, step, on):
                    nxt, g, c, f, done = (Group(pair, step + k) for k in (1, 0, -1, -2, -3))
                    if on["channel"]:
                        channel_k(c, 0)
                        channel_k(c, 1)
                    if on["store"]:
                        last_product(done)
                    if on["channel"]:
                        channel_k(c, 2)
                    if on["store"]:
                        turn_5(done)
                    if on["channel"]:
                        channel_k(c, 3)
                        channel_v(c)
                    if on["ffn"]:
                        gate_products(f, 0)
                        gate_products(f, 1)
                    if on["shift_k"]:
                        turn_1(nxt)
                    if on["ffn"]:
                        gate_products(f, 2)
                        gate_products(f, 3)
                    if on["channel"]:
                        spikes_turned(1, c)
                    if on["wkv"]:
                        out_product(g)
                    if on["ffn"]:
                        hidden(1, f, 0)
                        hidden(1, f, 1)
                        hidden(1, f, 2)
                    if on["wkv"]:
                        spikes_turned(0, g)
                    if on["ffn"]:
                        hidden(1, f, 3)
                    if on["shift_k"]:
                        k_product(nxt)
                        v_r_products(nxt)
                    if on["ffn"]:
                        hidden(2, f, 0)
                        hidden(2, f, 1)
                    if on["wkv"]:
                        turn_2(g)
                    if on["ffn"]:
                        hidden(2, f, 2)
                        hidden(2, f, 3)
                    if on["channel"]:
                        turn_4(c)
                    if on["wkv"]:
                        r_product(g)

                schedule(pe.Fori, turn, **turns)

            program(False, last=1)
            pe.wait_ge(s_hi_w, len(parts))
            pe.wait_ge(s_lo_w, len(parts))
            pe.wait_ge(s_rest_all, 1)
            long_weights = pe.value_load(w_rest_all[0:1, 0:1].bitcast(I32))
            with pe.If(long_weights != 0):
                program(True, first=2)
            with pe.Else():
                program(False, first=2)


def kernel(**inputs):
    import numpy as np
    import concourse.bacc as bacc
    from concourse.bass_utils import run_bass_kernel_spmd

    a = {k[len("L0_attn_"):]: np.asarray(v) for k, v in inputs.items() if k.startswith("L0_attn_")}
    f = {k[len("L0_ffn_"):]: np.asarray(v) for k, v in inputs.items() if k.startswith("L0_ffn_")}
    hb = f["w1_w"].shape[0] // P

    def rows(w):
        return w.reshape(-1, P, w.shape[1]).transpose(1, 0, 2)

    def blocks(w):
        return w.reshape(w.shape[0] // P, P, w.shape[1] // P, P).transpose(3, 0, 2, 1).reshape(P, -1, P)

    arrays = {
        "x": a["x"],
        "vec": np.stack([{**a, **f}[n] for n in VECTORS], axis=1),
        "scale": np.stack([f[n].reshape(hb, P).T for n in ("w1_s", "w2_s", "h1_s", "h2_s")], axis=1),
        "mix": np.concatenate([a[n][:, None, :] for n in ("Wk", "Wv", "Wr", "Wo", "fWr")]
                              + [a["fWk"].reshape(P, hb, P), rows(a["fWv"])], axis=1),
        "ffn": np.concatenate([blocks(f[n]) for n in ("h1_w", "h2_w", "w1_w", "w2_w", "w3_w")], axis=1),
    }
    arrays = {f"in_{k}": np.ascontiguousarray(v) for k, v in arrays.items()}
    nc = bacc.Bacc("TRN2", target_bir_lowering=False, num_devices=1)
    args = [nc.dram_tensor(k, v.shape, mybir.dt.from_np(v.dtype), kind="ExternalInput").ap() for k, v in arrays.items()]
    shape = arrays["in_x"].shape
    out = nc.dram_tensor("out", shape, F32, kind="ExternalOutput").ap()
    build(nc, *args, out)
    r = run_bass_kernel_spmd(nc, [arrays], core_ids=[0])
    return r.results[0]["out"]
```

```python
from contextlib import ExitStack

import concourse.bass as bass
from concourse import mybir

F32 = mybir.dt.float32
F32R = mybir.dt.float32r
BF16 = mybir.dt.bfloat16
I32 = mybir.dt.int32
ALU = mybir.AluOpType
ACT = mybir.ActivationFunctionType
AX_X = mybir.AxisListType.X
RMAX = bass.bass_isa.ReduceOp.max

P = 128
EPS = 1e-5
NO_MAXIMUM = -1e38

VECTORS = ["ln1_s", "ln1_b", "ln2_s", "ln2_b", "tmk", "tmv", "tmr", "w_decay", "u_first", "f_tmk", "f_tmr",
           "w3_s"]
VEC = {name: n for n, name in enumerate(VECTORS)}
MIX = {"Wk": 0, "Wv": 1, "Wr": 2, "Wo": 3, "fWr": 4, "fWk": 5, "fWv": 9}
POOL_BLOCKS = {1: (1,), 2: (1,), 3: (1, 2)}


class Group:

    def __init__(self, pair, step):
        self.n = 2 * pair + step
        self.par = step % 2
        self.turn = pair + step // 2


def wait(eng, sem, count):
    if not isinstance(count, int) or count > 0:
        eng.wait_ge(sem, count)


def build(nc, x_in, vec_in, scale_in, mix_in, ffn_in, out):
    B, T, C = x_in.shape
    NB = 2
    N = NB * T
    J = N // P
    GROUPS = B // NB
    MB = ffn_in.shape[1]
    HB = scale_in.shape[2]
    assert C == P and N == 512 and 3 * HB + 2 * HB * HB == MB and GROUPS % 2 == 0
    H1, H2, W1, W2, W3 = 0, HB * HB, 2 * HB * HB, 2 * HB * HB + HB, 2 * HB * HB + 2 * HB

    x_tiles = x_in.rearrange("(g b) (h p) c -> g p (b h) c", b=NB, p=P)
    out_tiles = out.rearrange("(g b) (h p) c -> g p (b h) c", b=NB, p=P)

    with ExitStack() as ctx:
        def sb(name, shape, dt=F32):
            return ctx.enter_context(nc.sbuf_tensor(name, shape, dt))

        def bank(name, dt=F32, shape=(P, 512)):
            return ctx.enter_context(nc.psum_tensor(name, list(shape), dt))

        def sem(name):
            return ctx.enter_context(nc.semaphore(name))

        vec = sb("vec", [P, len(VECTORS)])
        scale = sb("scale", [P, 4, HB])
        mix = sb("mix", [P, mix_in.shape[1], P])
        w_hi = sb("w_hi", [P, MB, P], F32R)
        w_lo = sb("w_lo", [P, MB, P], F32R)
        w_rest = sb("w_rest", [P, 3])
        w_rest1 = sb("w_rest1", [P, 1])
        w_rest_all = sb("w_rest_all", [P, 1])
        neg_decay = sb("neg_decay", [P, 1])
        pos_decay = sb("pos_decay", [P, 1])
        u_plus_w = sb("u_plus_w", [P, 1])
        decay_row = sb("decay_row", [P, T])
        half_row = sb("half_row", [P, T])
        minus_half = sb("minus_half", [P, 2, J])
        minus_one = sb("minus_one", [P, J])
        neg_mean = {n: sb(f"neg_mean{n}", [P, J]) for n in (1, 3, 5)}
        eps_row = sb("eps_row", [P, J])
        ident = sb("ident", [P, P])
        ident16 = sb("ident16", [P, P], BF16)

        xa = sb("xa", [P, 2, J, C])
        x1 = sb("x1", [P, 2, J, C])
        n1 = sb("n1", [P, J, C])
        bn1 = sb("bn1", [P, J, 6])
        mv1 = sb("mv1", [P, J, 2])
        var1 = sb("var1", [P, 2, J])
        rstd1 = sb("rstd1", [P, 2, J])
        z1 = sb("z1", [P, NB, T + 1])
        d1 = sb("d1", [P, NB, T])
        mixed1 = sb("mixed1", [P, 3, NB, T])
        o = sb("o", [P, NB, T + 1])
        e = sb("e", [P, NB, T])
        factors = sb("factors", [P, 4, NB, T])
        tanh_r = sb("tanh_r", [P, NB, T])
        bv = sb("bv", [P, 2, NB, T])
        pq = sb("pq", [P, 2, NB, T + 1])
        nd = sb("nd", [P, 2, NB, T])
        y = sb("y", [P, NB, T])
        yr = sb("yr", [P, NB, T])
        h_in = [sb(f"h_in{k}", [P, NB, T]) for k in range(2)]
        volt = [sb(f"volt{k}", [P, NB, T]) for k in range(2)]
        spikes = [sb(f"spikes{k}", [P, NB, T], BF16) for k in range(2)]
        fired = [sb(f"fired{k}", [P, 1]) for k in range(2)]
        fired_all = [sb(f"fired_all{k}", [P, 1]) for k in range(2)]
        cell = sb("cell", [P, NB])
        cell_mask = sb("cell_mask", [P, NB])
        half_cell = sb("half_cell", [P, NB])
        x2 = sb("x2", [P, 2, J, C])
        n2 = sb("n2", [P, J, C])
        bn2 = sb("bn2", [P, J, 6])
        mv2 = sb("mv2", [P, J, 2])
        var2 = sb("var2", [P, J])
        rstd2 = sb("rstd2", [P, J])
        z2 = sb("z2", [P, NB, T + 1])
        d2 = sb("d2", [P, NB, T])
        mixed2 = sb("mixed2", [P, 2, NB, T])
        tanh_r2 = sb("tanh_r2", [P, NB, T])
        kk = sb("kk", [P, HB, N])
        xb = sb("xb", [P, 2, J, C])
        x3 = sb("x3", [P, J, C])
        bn3 = sb("bn3", [P, J, 6])
        mv3 = sb("mv3", [P, J, 2])
        var3 = sb("var3", [P, J])
        rstd3 = sb("rstd3", [P, J])
        n3 = sb("n3", [P, J, C])
        xres = sb("xres", [P, 2, J, C])
        bn4 = sb("bn4", [P, J, 6])
        mv4 = sb("mv4", [P, J, 2])
        var4 = sb("var4", [P, J])
        rstd4 = sb("rstd4", [P, J])
        n4 = sb("n4", [P, J, C])
        f0_hi = sb("f0_hi", [P, 1, N], F32R)
        f0_lo = sb("f0_lo", [P, 1, N], F32R)
        gate = sb("gate", [P, 2, N])
        hid = sb("hid", [P, HB, N])
        ac_hi = sb("ac_hi", [P, HB, N], F32R)
        ac_lo = sb("ac_lo", [P, HB, N], F32R)
        b_hi = sb("b_hi", [P, HB, N], F32R)
        b_lo = sb("b_lo", [P, HB, N], F32R)
        f_cm = sb("f_cm", [P, N])
        f_out = sb("f_out", [P, J, C])
        bn5 = sb("bn5", [P, J, 6])
        mv5 = sb("mv5", [P, J, 2])
        var5 = sb("var5", [P, J])
        rstd5 = sb("rstd5", [P, J])
        y_out = sb("y_out", [P, J, C])

        p_turn = bank("p_turn")
        p_spk = bank("p_spk", BF16, (P, 2, 512))
        p_k = bank("p_k")
        p_v = bank("p_v")
        p_m = [bank(f"p_m{k}") for k in range(2)]
        p_f = [bank(f"p_f{k}") for k in range(2)]

        s_vec_in = sem("s_vec_in")
        s_mix_in = sem("s_mix_in")
        s_channel_in = sem("s_channel_in")
        s_stage = [sem(f"s_stage{k}") for k in range(2)]
        s_pool_const = sem("s_pool_const")
        s_ident0 = sem("s_ident0")
        s_pos = sem("s_pos")
        s_vec = sem("s_vec")
        s_hi_w = sem("s_hi_w")
        s_lo_w = sem("s_lo_w")
        s_rest = sem("s_rest")
        s_rest1 = sem("s_rest1")
        s_quarter = sem("s_quarter")
        s_rest_all = sem("s_rest_all")
        s_xa = [sem(f"s_xa{k}") for k in range(2)]
        s_xb = [sem(f"s_xb{k}") for k in range(2)]
        s_bn = {n: sem(f"s_bn{n}") for n in (1, 2, 3, 4, 5)}
        s_mv = {n: sem(f"s_mv{n}") for n in (1, 2, 3, 4, 5)}
        s_x1 = sem("s_x1")
        s_n = {n: sem(f"s_n{n}") for n in (1, 2, 3, 4, 5)}
        s_turned = {n: sem(f"s_turned{n}") for n in (1, 2, 4, 5)}
        s_z1 = sem("s_z1")
        s_d1 = sem("s_d1")
        s_mixed1 = sem("s_mixed1")
        s_k = sem("s_k")
        s_v = sem("s_v")
        s_r = sem("s_r")
        s_o = sem("s_o")
        s_e = sem("s_e")
        s_bounds = sem("s_bounds")
        s_under = sem("s_under")
        s_tanh_r = sem("s_tanh_r")
        s_expA = sem("s_expA")
        s_expB = sem("s_expB")
        s_bv = sem("s_bv")
        s_pq = sem("s_pq")
        s_apq = sem("s_apq")
        s_den = sem("s_den")
        s_num = sem("s_num")
        s_ln = sem("s_ln")
        s_inv = sem("s_inv")
        s_yr = sem("s_yr")
        s_y = sem("s_y")
        s_wo = sem("s_wo")
        s_h_in = [sem(f"s_h_in{k}") for k in range(2)]
        s_volt = [sem(f"s_volt{k}") for k in range(2)]
        s_fired = [sem(f"s_fired{k}") for k in range(2)]
        s_spikes = [sem(f"s_spikes{k}") for k in range(2)]
        s_fired_all = [sem(f"s_fired_all{k}") for k in range(2)]
        s_spk_tok = [sem(f"s_spk_tok{k}") for k in range(2)]
        s_x2 = sem("s_x2")
        s_z2 = sem("s_z2")
        s_d2 = sem("s_d2")
        s_mixed2 = sem("s_mixed2")
        s_r2 = sem("s_r2")
        s_tanh_r2 = sem("s_tanh_r2")
        s_fk = sem("s_fk")
        s_relu = sem("s_relu")
        s_square = sem("s_square")
        s_fv = sem("s_fv")
        s_x3 = sem("s_x3")
        s_xres = sem("s_xres")
        s_f0_hi = sem("s_f0_hi")
        s_f0_lo = sem("s_f0_lo")
        s_ab = sem("s_ab")
        s_gate = sem("s_gate")
        s_swiglu = sem("s_swiglu")
        s_h = {1: sem("s_h1"), 2: sem("s_h2")}
        s_gelu = {1: sem("s_gelu1"), 2: sem("s_gelu2")}
        s_hi = {n: sem(f"s_hi{n}") for n in (1, 2, 3)}
        s_lo = {n: sem(f"s_lo{n}") for n in (1, 2, 3)}
        s_lo_pool = {n: sem(f"s_lo_pool{n}") for n in (1, 2, 3)}
        s_w3 = sem("s_w3")
        s_f_cm = sem("s_f_cm")
        s_f_out = sem("s_f_out")
        s_y_out = sem("s_y_out")
        s_stored = sem("s_stored")
        s_var = {n: sem(f"s_var{n}") for n in (1, 2, 3, 4, 5)}
        s_neg_mean = {n: sem(f"s_neg_mean{n}") for n in (1, 3, 5)}
        s_rstd = {n: sem(f"s_rstd{n}") for n in (1, 2, 3, 4, 5)}

        s_apart = sem("s_apart")

        def apart(eng):
            eng.sem_inc(s_apart, 1)

        def low_ready(eng, layer, g, m):
            others = [k for k in range(HB) if k not in POOL_BLOCKS[layer]]
            if m in POOL_BLOCKS[layer]:
                eng.wait_ge(s_lo_pool[layer], len(POOL_BLOCKS[layer]) * g.n + POOL_BLOCKS[layer].index(m) + 1)
            else:
                eng.wait_ge(s_lo[layer], len(others) * g.n + others.index(m) + 1)

        def split_low(eng, layer, g, m):
            hi, lo = (b_hi, b_lo) if layer == 2 else (ac_hi, ac_lo)
            eng.wait_ge(s_hi[layer], HB * g.n + m + 1)
            done = (s_lo_pool if m in POOL_BLOCKS[layer] else s_lo)[layer]
            eng.tensor_tensor(lo[:, m], hid[:, m], hi[:, m].bitcast(F32), ALU.subtract).then_inc(done, 1)

        def col(name):
            return vec[:, VEC[name]:VEC[name] + 1]

        def flat(t):
            return t.rearrange("p b t -> p (b t)")

        parts = [(kk, H1, HB * HB), (hid, H2, HB * HB), (hid, W1, 3 * HB)]

        def part(n):
            buffer, first, count = parts[n]
            staged = buffer[:, :, :].rearrange("p h (b c) -> p (h b) c", c=P)
            return staged[:, 0:count], slice(first, first + count)

        block = ctx.enter_context(nc.Block())

        def schedule(fori, first_turn, turn, last_turn, first=-1, last=GROUPS + 2):
            def on(i):
                return {"shift_k": i + 1 < GROUPS, "wkv": 0 <= i < GROUPS, "channel": 0 <= i - 1 < GROUPS,
                        "ffn": 0 <= i - 2 < GROUPS, "store": 0 <= i - 3 < GROUPS, "weights": i + 1 < len(parts)}
            loop = range(4, GROUPS - 2)
            for i in range(first, last + 1):
                if i == loop[0]:
                    with fori(loop[0] // 2, len(loop) // 2 + loop[0] // 2) as pair:
                        turn(pair, 0, on(4))
                        turn(pair, 1, on(5))
                elif i not in loop:
                    which = first_turn if i < 2 else turn if i < GROUPS else last_turn
                    which(i // 2, i % 2, on(i))

        @block.sync
        def _(sp):
            def load_a(g):
                wait(sp, s_x1, g.n - 1)
                wait(sp, s_n[1], g.n - 1)
                sp.dma_start(xa[:, g.par], x_tiles[g.n]).then_inc(s_xa[g.par], 16)

            def load_b(g):
                wait(sp, s_xres, g.n - 1)
                sp.dma_start(xb[:, g.par], x_tiles[g.n]).then_inc(s_xb[g.par], 16)

            def load_weights(n):
                staged, blocks = part(n)
                if n == 2:
                    sp.wait_ge(s_rest, n)
                sp.dma_start(staged, ffn_in[:, blocks]).then_inc(s_stage[min(n, 1)], 16)

            load_a(Group(0, 0))
            sp.dma_start(vec[:, :], vec_in).then_inc(s_vec_in, 16)
            split = MIX["fWk"]
            sp.dma_start(mix[:, 0:split], mix_in[:, 0:split]).then_inc(s_mix_in, 16)
            load_weights(0)
            sp.dma_start(mix[:, split:], mix_in[:, split:]).then_inc(s_channel_in, 16)
            sp.dma_start(scale[:, :, :], scale_in).then_inc(s_channel_in, 16)
            load_weights(1)
            load_a(Group(0, 1))
            load_b(Group(0, 0))
            load_a(Group(0, 2))
            load_weights(2)

            def turn(pair, step, on):
                g = Group(pair, step)
                if not isinstance(g.n, int) or 1 <= g.n < GROUPS - 2:
                    load_a(Group(pair, step + 2))
                if on["wkv"] and (not isinstance(g.n, int) or g.n > 0):
                    load_b(g)
                if on["store"]:
                    f = Group(pair, step - 3)
                    sp.wait_ge(s_y_out, f.n + 1)
                    sp.dma_start(out_tiles[f.n], y_out[:, :, :]).then_inc(s_stored, 16)

            schedule(sp.Fori, turn, turn, turn)
            sp.wait_ge(s_stored, 16 * GROUPS)

        @block.gpsimd
        def _(pool):
            pool.memset(ident[:, :], 0.0).then_inc(s_ident0, 1)
            pool.memset(half_row[:, :], 0.5).then_inc(s_pool_const, 1)
            pool.memset(minus_half[:, :, :], -0.5).then_inc(s_pool_const, 1)
            pool.memset(minus_one[:, :], -1.0).then_inc(s_pool_const, 1)
            pool.memset(eps_row[:, :], EPS).then_inc(s_pool_const, 1)
            pool.memset(half_cell[:, :], 0.5).then_inc(s_pool_const, 1)
            pool.memset(z1[:, :, 0:1], 0.0).then_inc(s_pool_const, 1)
            pool.memset(z2[:, :, 0:1], 0.0).then_inc(s_pool_const, 1)
            pool.memset(o[:, :, 0:1], NO_MAXIMUM).then_inc(s_pool_const, 1)
            pool.memset(pq[:, :, :, 0:1], 0.0).then_inc(s_pool_const, 1)
            pool.wait_ge(s_ident0, 1)
            pool.affine_select(out=ident[:, :], in_=ident[:, :], compare_op=ALU.not_equal, fill=1.0, base=0,
                               pattern=[[-1, P]], channel_multiplier=1).then_inc(s_pool_const, 1)
            pool.wait_ge(s_pool_const, 10)

            mv, var = {2: mv2, 3: mv3, 4: mv4, 5: mv5}, {2: var2, 3: var3, 4: var4, 5: var5}
            rstds = {2: rstd2, 3: rstd3, 4: rstd4, 5: rstd5}

            def variance(n, g):
                pool.wait_ge(s_mv[n], g.n + 1)
                wait(pool, s_rstd[n], g.n)
                if n == 1:
                    apart(pool)
                    pool.tensor_scalar(var1[:, 0], mv1[:, :, 1], 1.0, EPS, ALU.mult, ALU.add).then_inc(s_var[1], 1)
                    pool.tensor_scalar(var1[:, 1], mv1[:, :, 1], 1.0 + EPS, EPS * EPS, ALU.mult,
                                       ALU.add).then_inc(s_var[1], 1)
                else:
                    pool.tensor_tensor(var[n][:, :], mv[n][:, :, 1], eps_row[:, :], ALU.add).then_inc(s_var[n], 1)
                if n in neg_mean:
                    pool.tensor_tensor(neg_mean[n][:, :], (mv1 if n == 1 else mv[n])[:, :, 0], minus_one[:, :],
                                       ALU.mult).then_inc(s_neg_mean[n], 1)

            def rstd(n, g):
                if n == 1:
                    pool.wait_ge(s_var[1], 2 * (g.n + 1))
                    pool.tensor_tensor(rstd1[:, :, :], var1[:, :, :], minus_half[:, :, :],
                                       ALU.pow).then_inc(s_rstd[1], 1)
                else:
                    pool.wait_ge(s_var[n], g.n + 1)
                    pool.tensor_tensor(rstds[n][:, :], var[n][:, :], minus_half[:, 0], ALU.pow).then_inc(s_rstd[n], 1)

            def centered(n, g, out_, in_, rstd):
                pool.wait_ge(s_neg_mean[n], g.n + 1)
                pool.wait_ge(s_rstd[n], g.n + 1)
                apart(pool)
                for j in range(J):
                    last = pool.tensor_scalar(out_[:, j], in_[:, j], neg_mean[n][:, j:j + 1], rstd[:, j:j + 1], ALU.add,
                                              ALU.mult)
                return last

            def long_weights(i):
                if i + 2 == len(parts):
                    pool.wait_ge(s_rest1, 1)
                    pool.partition_all_reduce(w_rest_all[:, :], w_rest1[:, :], P, RMAX).then_inc(s_rest_all, 1)

            def weighted_sum(g, n):
                wait(pool, s_yr, g.n)
                pool.wait_ge(s_pq, 2 * (g.n + 1) - n)
                pool.tensor_tensor(nd[:, n], factors[:, 0], pq[:, n, :, 0:T], ALU.mult).then_inc(s_apq, 1)

            def shift_1(g):
                pool.wait_ge(s_z1, g.n + 1)
                wait(pool, s_mixed1, 3 * g.n)
                pool.tensor_tensor(d1[:, :, :], z1[:, :, 1:T + 1], z1[:, :, 0:T], ALU.subtract).then_inc(s_d1, 1)

            def shift_2(g):
                pool.wait_ge(s_z2, g.n + 1)
                wait(pool, s_mixed2, 2 * g.n)
                pool.tensor_tensor(d2[:, :, :], z2[:, :, 1:T + 1], z2[:, :, 0:T], ALU.subtract).then_inc(s_d2, 1)

            def neurons(k, g):
                pool.wait_ge(s_fired[k], g.n + 1)
                pool.wait_ge(s_h_in[k], g.n + 1)
                apart(pool)
                pool.partition_all_reduce(fired_all[k][:, :], fired[k][:, :], P, RMAX).then_inc(s_fired_all[k], 1)
                pool.wait_ge(s_fired_all[k], g.n + 1)
                apart(pool)
                any_spike = pool.value_load(fired_all[k][0:1, 0:1].bitcast(I32))
                with pool.If(any_spike != 0):
                    pool.memset(cell[:, :], 0.0)
                    pool.drain()
                    with pool.Fori(0, T) as t:
                        x_t = h_in[k][:, :, bass.ds(t, 1)].rearrange("p b o -> p (b o)")
                        spikes_t = spikes[k][:, :, bass.ds(t, 1)].rearrange("p b o -> p (b o)")
                        pool.tensor_tensor(cell[:, :], cell[:, :], half_cell[:, :], ALU.mult)
                        pool.drain()
                        pool.tensor_tensor(cell[:, :], cell[:, :], x_t, ALU.add)
                        pool.drain()
                        pool.tensor_scalar(cell_mask[:, :], cell[:, :], 1.0, None, ALU.is_ge)
                        pool.drain()
                        pool.tensor_copy(spikes_t, cell_mask[:, :])
                        pool.tensor_scalar(cell_mask[:, :], cell_mask[:, :], -1.0, 1.0, ALU.mult, ALU.add)
                        pool.drain()
                        pool.tensor_tensor(cell[:, :], cell[:, :], cell_mask[:, :], ALU.mult)
                        pool.drain()
                pool.engine_nop().then_inc(s_spikes[k], 1)

            def norm_0(g):
                wait(pool, s_x2, g.n - 1)
                centered(1, g, x1[:, g.par], xa[:, g.par], rstd1[:, 0]).then_inc(s_x1, 1)

            def norm_3(g):
                wait(pool, s_xres, g.n)
                centered(3, g, n3, x3, rstd3).then_inc(s_n[3], 1)

            def norm_5(g):
                centered(5, g, f_out, f_out, rstd5).then_inc(s_n[5], 1)

            def residual_3(g):
                pool.wait_ge(s_xb[g.par], 16 * (g.turn + 1))
                wait(pool, s_y_out, g.n - 1)
                pool.wait_ge(s_n[3], g.n + 1)
                pool.tensor_tensor(xres[:, g.par], xb[:, g.par], n3[:, :, :], ALU.add).then_inc(s_xres, 1)

            def residual_5(g):
                wait(pool, s_stored, 16 * g.n)
                pool.wait_ge(s_n[5], g.n + 1)
                pool.tensor_tensor(y_out[:, :, :], f_out[:, :, :], xres[:, g.par], ALU.add).then_inc(s_y_out, 1)

            def low(layer, g, m):
                split_low(pool, layer, g, m)

            def first_turn(pair, step, on):
                nxt, g, c = (Group(pair, step + k) for k in (1, 0, -1))
                if on["shift_k"]:
                    variance(1, nxt)
                    rstd(1, nxt)
                if on["wkv"]:
                    weighted_sum(g, 1)
                    weighted_sum(g, 0)
                if on["channel"]:
                    neurons(1, c)
                if on["shift_k"]:
                    shift_1(nxt)
                if on["wkv"]:
                    neurons(0, g)
                if on["channel"]:
                    variance(3, c)
                    rstd(3, c)
                    norm_3(c)
                    residual_3(c)
                if on["wkv"]:
                    variance(2, g)
                    rstd(2, g)
                if on["channel"]:
                    variance(4, c)
                    rstd(4, c)
                if on["wkv"]:
                    shift_2(g)
                if on["shift_k"]:
                    norm_0(nxt)
                if on["weights"]:
                    long_weights(g.n)

            def turn(pair, step, on):
                nxt, g, c, f, done = (Group(pair, step + k) for k in (1, 0, -1, -2, -3))
                if on["shift_k"]:
                    variance(1, nxt)
                    rstd(1, nxt)
                if on["wkv"]:
                    weighted_sum(g, 1)
                    weighted_sum(g, 0)
                if on["store"]:
                    variance(5, done)
                    rstd(5, done)
                    norm_5(done)
                if on["shift_k"]:
                    shift_1(nxt)
                if on["channel"]:
                    neurons(1, c)
                if on["ffn"]:
                    low(1, f, 1)
                if on["store"]:
                    residual_5(done)
                if on["wkv"]:
                    neurons(0, g)
                if on["channel"]:
                    variance(3, c)
                if on["ffn"]:
                    low(2, f, 1)
                if on["channel"]:
                    rstd(3, c)
                if on["wkv"]:
                    variance(2, g)
                    rstd(2, g)
                if on["channel"]:
                    norm_3(c)
                    residual_3(c)
                if on["wkv"]:
                    shift_2(g)
                if on["channel"]:
                    variance(4, c)
                    rstd(4, c)
                if on["shift_k"]:
                    norm_0(nxt)
                if on["ffn"]:
                    low(3, f, 1)
                    low(3, f, 2)

            def last_turn(pair, step, on):
                c, f, done = (Group(pair, step + k) for k in (-1, -2, -3))
                if on["store"]:
                    variance(5, done)
                if on["ffn"]:
                    low(1, f, 1)
                if on["store"]:
                    rstd(5, done)
                    norm_5(done)
                if on["channel"]:
                    neurons(1, c)
                if on["ffn"]:
                    low(2, f, 1)
                if on["store"]:
                    residual_5(done)
                if on["channel"]:
                    variance(3, c)
                    rstd(3, c)
                    norm_3(c)
                    residual_3(c)
                    variance(4, c)
                    rstd(4, c)
                if on["ffn"]:
                    low(3, f, 1)
                    low(3, f, 2)

            schedule(pool.Fori, first_turn, turn, last_turn)

        @block.scalar
        def _(act):
            act.wait_ge(s_vec_in, 16)
            act.activation(pos_decay[:, :], col("w_decay"), ACT.Exp).then_inc(s_pos, 1)
            act.wait_ge(s_vec, 2)

            def high_weights(i):
                staged, blocks = part(i + 1)
                act.wait_ge(s_stage[min(i + 1, 1)], 16 * max(i + 1, 1))
                act.activation(w_hi[:, blocks], staged, ACT.Copy).then_inc(s_hi_w, 1)

            def z_1(g):
                act.wait_ge(s_turned[1], g.n + 1)
                if isinstance(g.n, int) and g.n == 0:
                    act.wait_ge(s_pool_const, 10)
                wait(act, s_mixed1, 3 * g.n)
                act.activation(z1[:, :, 1:T + 1], p_turn[:, :].rearrange("p (b t) -> p b t", b=NB), ACT.Identity,
                               bias=col("ln1_b"), scale=col("ln1_s")).then_inc(s_z1, 1)

            def tanh_1(g):
                act.wait_ge(s_r, g.n + 1)
                wait(act, s_y, g.n)
                act.activation(flat(tanh_r[:, :, :]), p_m[0][:, :], ACT.Tanh, scale=0.5).then_inc(s_tanh_r, 1)

            def under(g, n):
                act.wait_ge(s_e, g.n + 1)
                wait(act, s_num, g.n)
                wait(act, s_den, g.n)
                act.activation(factors[:, 2 + n], e[:, :, :], ACT.Relu, scale=-1.0,
                               **({"bias": u_plus_w[:, 0:1]} if n else {})).then_inc(s_under, 1)

            def exp_table(g):
                act.preload_act_table_set("natural_log_exp_and_others")

            def silu_table(g):
                act.preload_act_table_set("silu_and_others")

            def gelu_table(g):
                act.preload_act_table_set("gelu_and_others")

            def exps(g, n):
                if n == 0:
                    act.wait_ge(s_bounds, 2 * (g.n + 1))
                    act.activation(factors[:, 0:2], factors[:, 0:2], ACT.Exp, scale=-1.0).then_inc(s_expA, 1)
                else:
                    act.wait_ge(s_under, 2 * (g.n + 1))
                    act.activation(factors[:, 2:4], factors[:, 2:4], ACT.Exp, scale=-1.0).then_inc(s_expB, 1)

            def log(g):
                act.wait_ge(s_den, g.n + 1)
                wait(act, s_yr, g.n)
                act.activation(y[:, :, :], nd[:, 1], ACT.Ln).then_inc(s_ln, 1)

            def inverse(g):
                act.wait_ge(s_ln, g.n + 1)
                act.activation(y[:, :, :], y[:, :, :], ACT.Exp, scale=-1.0).then_inc(s_inv, 1)

            def neuron_input_1(g):
                act.wait_ge(s_wo, g.n + 1)
                wait(act, s_spikes[0], g.n)
                act.activation(flat(h_in[0][:, :, :]), p_k[:, :], ACT.Copy).then_inc(s_h_in[0], 1)

            def z_2(g):
                act.wait_ge(s_turned[2], g.n + 1)
                wait(act, s_mixed2, 2 * g.n)
                act.activation(z2[:, :, 1:T + 1], p_turn[:, :].rearrange("p (b t) -> p b t", b=NB), ACT.Identity,
                               bias=col("ln2_b"), scale=col("ln2_s")).then_inc(s_z2, 1)

            def tanh_2(g):
                act.wait_ge(s_r2, g.n + 1)
                wait(act, s_h_in[1], g.n)
                act.activation(flat(tanh_r2[:, :, :]), p_m[1][:, :], ACT.Tanh, scale=0.5).then_inc(s_tanh_r2, 1)

            def relu(g, m):
                act.wait_ge(s_fk, HB * g.n + m + 1)
                wait(act, s_fv, g.n)
                if isinstance(g.n, int) and g.n == 0:
                    act.wait_ge(s_rest, 1)
                act.activation(kk[:, m], p_m[m % 2][:, :], ACT.Relu).then_inc(s_relu, 1)

            def square(g, m):
                act.wait_ge(s_relu, HB * g.n + m + 1)
                act.activation(kk[:, m], kk[:, m], ACT.Square).then_inc(s_square, 1)

            def f0(g):
                act.wait_ge(s_turned[4], g.n + 1)
                wait(act, s_ab, 2 * HB * g.n)
                act.activation(f0_hi[:, 0], p_turn[:, :], ACT.Copy).then_inc(s_f0_hi, 1)

            def silu(g, m):
                if isinstance(g.n, int) and g.n == 0:
                    act.wait_ge(s_channel_in, 32)
                act.wait_ge(s_ab, 2 * HB * g.n + 2 * m + 1)
                wait(act, s_swiglu, HB * g.n + max(m - 1, 0))
                act.activation(gate[:, m % 2], (p_v if m % 2 else p_f[0])[:, :], ACT.Silu,
                               scale=scale[:, 0, m:m + 1]).then_inc(s_gate, 1)

            def high(layer, g, m):
                act.wait_ge(s_swiglu if layer == 1 else s_gelu[layer - 1], HB * g.n + m + 1)
                if layer == 1:
                    wait(act, s_w3, g.n)
                elif layer == 2:
                    wait(act, s_h[2], HB * g.n)
                else:
                    act.wait_ge(s_h[1], HB * (g.n + 1))
                dst = b_hi if layer == 2 else ac_hi
                act.activation(dst[:, m], hid[:, m], ACT.Copy).then_inc(s_hi[layer], 1)

            def gelu(layer, g, m):
                act.wait_ge(s_h[layer], HB * g.n + m + 1)
                low_ready(act, layer, g, m)
                act.activation(hid[:, m], p_f[m % 2][:, :], ACT.Gelu,
                               scale=scale[:, 1 + layer, m:m + 1]).then_inc(s_gelu[layer], 1)

            def output_scaled(g):
                act.wait_ge(s_w3, g.n + 1)
                wait(act, s_turned[5], g.n)
                act.activation(f_cm[:, :], p_f[0][:, :], ACT.Copy, scale=col("w3_s")).then_inc(s_f_cm, 1)

            def output_tokens(g):
                act.wait_ge(s_turned[5], g.n + 1)
                wait(act, s_y_out, g.n)
                act.activation(f_out[:, :, :], p_turn[:, :].rearrange("p (j c) -> p j c", c=C),
                               ACT.Copy).then_inc(s_f_out, 1)

            def first_turn(pair, step, on):
                nxt, g, c = (Group(pair, step + k) for k in (1, 0, -1))
                if on["wkv"]:
                    exp_table(g)
                    exps(g, 1)
                if on["channel"]:
                    relu(c, 0)
                if on["wkv"]:
                    exps(g, 0)
                if on["channel"]:
                    relu(c, 1)
                    relu(c, 2)
                    square(c, 0)
                    square(c, 1)
                    relu(c, 3)
                    square(c, 2)
                    square(c, 3)
                if on["wkv"]:
                    log(g)
                    inverse(g)
                if on["weights"]:
                    high_weights(g.n)
                if on["shift_k"]:
                    z_1(nxt)
                if on["wkv"]:
                    neuron_input_1(g)
                if on["shift_k"]:
                    tanh_1(nxt)
                if on["wkv"]:
                    z_2(g)
                if on["shift_k"]:
                    under(nxt, 0)
                    under(nxt, 1)
                if on["wkv"]:
                    tanh_2(g)
                if on["channel"]:
                    f0(c)

            def turn(pair, step, on):
                nxt, g, c, f, done = (Group(pair, step + k) for k in (1, 0, -1, -2, -3))
                if on["wkv"]:
                    exp_table(g)
                    exps(g, 1)
                if on["channel"]:
                    relu(c, 0)
                if on["wkv"]:
                    exps(g, 0)
                if on["store"]:
                    output_scaled(done)
                if on["channel"]:
                    relu(c, 1)
                    relu(c, 2)
                    square(c, 0)
                    square(c, 1)
                if on["store"]:
                    output_tokens(done)
                if on["channel"]:
                    square(c, 2)
                    relu(c, 3)
                if on["wkv"]:
                    log(g)
                if on["channel"]:
                    square(c, 3)
                if on["wkv"]:
                    inverse(g)
                if on["ffn"]:
                    silu_table(f)
                    silu(f, 0)
                if on["shift_k"]:
                    z_1(nxt)
                if on["ffn"]:
                    silu(f, 1)
                    high(1, f, 0)
                if on["wkv"]:
                    neuron_input_1(g)
                if on["ffn"]:
                    silu(f, 2)
                    high(1, f, 1)
                    silu(f, 3)
                    high(1, f, 2)
                    high(1, f, 3)
                    gelu_table(f)
                    gelu(1, f, 0)
                    high(2, f, 0)
                    gelu(1, f, 1)
                    high(2, f, 1)
                    gelu(1, f, 2)
                    high(2, f, 2)
                    gelu(1, f, 3)
                    high(2, f, 3)
                if on["shift_k"]:
                    under(nxt, 0)
                if on["ffn"]:
                    gelu(2, f, 0)
                    high(3, f, 0)
                    gelu(2, f, 1)
                if on["wkv"]:
                    z_2(g)
                if on["ffn"]:
                    high(3, f, 1)
                if on["shift_k"]:
                    under(nxt, 1)
                if on["ffn"]:
                    gelu(2, f, 2)
                    high(3, f, 2)
                    gelu(2, f, 3)
                    high(3, f, 3)
                if on["shift_k"]:
                    tanh_1(nxt)
                if on["wkv"]:
                    tanh_2(g)
                if on["channel"]:
                    f0(c)

            def last_turn(pair, step, on):
                c, f, done = (Group(pair, step + k) for k in (-1, -2, -3))
                if on["channel"]:
                    relu(c, 0)
                if on["ffn"]:
                    silu_table(f)
                if on["channel"]:
                    square(c, 0)
                    relu(c, 1)
                if on["store"]:
                    output_scaled(done)
                if on["channel"]:
                    square(c, 1)
                    relu(c, 2)
                    relu(c, 3)
                    square(c, 2)
                if on["ffn"]:
                    silu(f, 0)
                if on["store"]:
                    output_tokens(done)
                if on["ffn"]:
                    silu(f, 1)
                    high(1, f, 0)
                    silu(f, 2)
                    high(1, f, 1)
                if on["channel"]:
                    square(c, 3)
                if on["ffn"]:
                    silu(f, 3)
                    high(1, f, 2)
                    high(1, f, 3)
                    gelu_table(f)
                    gelu(1, f, 0)
                    high(2, f, 0)
                    gelu(1, f, 1)
                    high(2, f, 1)
                    gelu(1, f, 2)
                    high(2, f, 2)
                    gelu(1, f, 3)
                    high(2, f, 3)
                    gelu(2, f, 0)
                    high(3, f, 0)
                    gelu(2, f, 1)
                    high(3, f, 1)
                    gelu(2, f, 2)
                    high(3, f, 2)
                    gelu(2, f, 3)
                    high(3, f, 3)
                if on["channel"]:
                    f0(c)

            schedule(act.Fori, first_turn, turn, last_turn)

        @block.vector
        def _(dve):
            dve.wait_ge(s_pos, 1)
            dve.tensor_scalar(neg_decay[:, :], pos_decay[:, :], -1.0, None, ALU.mult).then_inc(s_vec, 1)
            dve.wait_ge(s_vec, 1)
            dve.tensor_tensor(u_plus_w[:, :], col("u_first"), neg_decay[:, :], ALU.add).then_inc(s_vec, 1)
            dve.wait_ge(s_pool_const, 10)
            dve.tensor_scalar(decay_row[:, :], half_row[:, :], 0.0, neg_decay[:, 0:1], ALU.mult,
                              ALU.add).then_inc(s_vec, 1)
            dve.tensor_copy(ident16[:, :], ident[:, :]).then_inc(s_vec, 1)
            dve.wait_ge(s_vec, 4)

            def scaled_weights(i):
                if i < 0:
                    first, count = MIX["Wo"], 1
                    dve.wait_ge(s_mix_in, 16)
                elif i == 0:
                    first, count = MIX["fWv"], HB
                    dve.wait_ge(s_channel_in, 32)
                else:
                    return
                dve.tensor_scalar(mix[:, first:first + count], mix[:, first:first + count], 0.25, None,
                                  ALU.mult).then_inc(s_quarter, 1)

            def low_weights(i):
                staged, blocks = part(i + 1)
                dve.wait_ge(s_hi_w, i + 2)
                dve.tensor_tensor(w_lo[:, blocks], staged, w_hi[:, blocks].bitcast(F32),
                                  ALU.subtract).then_inc(s_lo_w, 1)

            def count_weights(i):
                staged, blocks = part(i + 1)
                dve.wait_ge(s_lo_w, i + 2)
                dve.tensor_scalar(staged, w_lo[:, blocks].bitcast(F32), 0.0, None, ALU.not_equal, ALU.add,
                                  accum_out=w_rest[:, i + 1:i + 2]).then_inc(s_rest, 1)
                if i + 2 == len(parts):
                    dve.wait_ge(s_rest, len(parts))
                    dve.tensor_reduce(w_rest1[:, :], w_rest[:, :], AX_X, ALU.max).then_inc(s_rest1, 1)

            def statistics(n, g, bn, tiles):
                for j in range(J):
                    last = dve.bn_stats(bn[:, j], tiles[:, j])
                last.then_inc(s_bn[n], 1)

            def moments(n, g, bn, mv):
                dve.wait_ge(s_bn[n], g.n + 1)
                apart(dve)
                for j in range(J):
                    last = dve.bn_aggr(mv[:, j], bn[:, j])
                last.then_inc(s_mv[n], 1)

            def stats_1(g):
                dve.wait_ge(s_xa[g.par], 16 * (g.turn + 1))
                statistics(1, g, bn1, xa[:, g.par])

            def moments_1(g):
                wait(dve, s_n[1], g.n)
                wait(dve, s_x1, g.n)
                moments(1, g, bn1, mv1)

            def centered(n, g, out_, in_, mv, rstd):
                dve.wait_ge(s_rstd[n], g.n + 1)
                for j in range(J):
                    last = dve.tensor_scalar(out_[:, j], in_[:, j], mv[:, j, 0:1], rstd[:, j:j + 1], ALU.subtract,
                                             ALU.mult)
                return last

            def norm_1(g):
                wait(dve, s_turned[1], g.n)
                centered(1, g, n1, xa[:, g.par], mv1, rstd1[:, 1]).then_inc(s_n[1], 1)

            def norm_2(g):
                wait(dve, s_turned[2], g.n)
                centered(2, g, n2, x2[:, g.par], mv2, rstd2).then_inc(s_n[2], 1)

            def norm_4(g):
                wait(dve, s_turned[4], g.n)
                centered(4, g, n4, xres[:, g.par], mv4, rstd4).then_inc(s_n[4], 1)

            def mix_1(g, n):
                dve.wait_ge(s_d1, g.n + 1)
                wait(dve, (s_k, s_v, s_r)[n], g.n)
                dve.scalar_tensor_tensor(mixed1[:, n], d1[:, :, :], col(("tmk", "tmv", "tmr")[n]), z1[:, :, 0:T],
                                         ALU.mult, ALU.add).then_inc(s_mixed1, 1)

            def maximum(g):
                dve.wait_ge(s_k, g.n + 1)
                for b in range(NB):
                    last = dve.tensor_tensor_scan(o[:, b, 1:T + 1], decay_row[:, :], p_k[:, b * T:(b + 1) * T],
                                                  NO_MAXIMUM, ALU.add, ALU.max)
                last.then_inc(s_o, 1)

            def excess(g):
                dve.wait_ge(s_o, g.n + 1)
                wait(dve, s_under, 2 * g.n)
                dve.scalar_tensor_tensor(e[:, :, :], p_k[:, :].rearrange("p (b t) -> p b t", b=NB), col("u_first"),
                                         o[:, :, 0:T], ALU.add, ALU.subtract).then_inc(s_e, 1)

            def bounds(g, n):
                dve.wait_ge(s_e, g.n + 1)
                wait(dve, s_num, g.n)
                wait(dve, s_den, g.n)
                if n == 0:
                    dve.tensor_scalar(factors[:, 0], e[:, :, :], 0.0, None, ALU.max).then_inc(s_bounds, 1)
                else:
                    dve.tensor_scalar(factors[:, 1], e[:, :, :], u_plus_w[:, 0:1], 0.0, ALU.subtract,
                                      ALU.max).then_inc(s_bounds, 1)

            def terms(g, n):
                dve.wait_ge(s_expB, g.n + 1)
                dve.wait_ge(s_v, g.n + 1)
                dve.tensor_tensor(flat(bv[:, n]), flat(factors[:, 2 + n]), p_v[:, :], ALU.mult).then_inc(s_bv, 1)

            def sum_over_time(g, n):
                dve.wait_ge(s_expA, g.n + 1)
                dve.wait_ge(s_expB, g.n + 1)
                wait(dve, s_apq, 2 * g.n)
                if n == 0:
                    dve.wait_ge(s_bv, 2 * (g.n + 1))
                new = factors[:, 3] if n else bv[:, 1]
                for b in range(NB):
                    last = dve.tensor_tensor_scan(pq[:, n, b, 1:T + 1], factors[:, 1, b], new[:, b], 0.0,
                                                  ALU.mult, ALU.add)
                last.then_inc(s_pq, 1)

            def denominator(g):
                dve.wait_ge(s_expB, g.n + 1)
                dve.wait_ge(s_apq, 2 * g.n + 1)
                dve.tensor_tensor(nd[:, 1], nd[:, 1], factors[:, 2], ALU.add).then_inc(s_den, 1)

            def numerator(g):
                dve.wait_ge(s_bv, 2 * (g.n + 1))
                dve.wait_ge(s_apq, 2 * g.n + 2)
                dve.tensor_tensor(nd[:, 0], nd[:, 0], bv[:, 0], ALU.add).then_inc(s_num, 1)

            def ratio(g):
                dve.wait_ge(s_num, g.n + 1)
                dve.wait_ge(s_tanh_r, g.n + 1)
                wait(dve, s_wo, g.n)
                dve.scalar_tensor_tensor(nd[:, 0], tanh_r[:, :, :], 1.0, nd[:, 0], ALU.add, ALU.mult).then_inc(s_y, 1)

            def ratio_end(g):
                dve.wait_ge(s_y, g.n + 1)
                dve.wait_ge(s_inv, g.n + 1)
                dve.tensor_tensor(yr[:, :, :], nd[:, 0], y[:, :, :], ALU.mult).then_inc(s_yr, 1)

            def voltage(k, g):
                dve.wait_ge(s_h_in[k], g.n + 1)
                for b in range(NB):
                    last = dve.tensor_tensor_scan(volt[k][:, b], half_row[:, :], h_in[k][:, b], 0.0, ALU.mult, ALU.add)
                last.then_inc(s_volt[k], 1)

            def fire(k, g):
                dve.wait_ge(s_volt[k], g.n + 1)
                wait(dve, s_spk_tok[k], g.n)
                wait(dve, s_spikes[k], g.n)
                dve.tensor_scalar(spikes[k][:, :, :], volt[k][:, :, :], 1.0, None, ALU.is_ge, ALU.add,
                                  accum_out=fired[k][:, :]).then_inc(s_fired[k], 1)

            def add_1(g):
                dve.wait_ge(s_spk_tok[0], g.n + 1)
                dve.wait_ge(s_x1, g.n + 1)
                wait(dve, s_x3, g.n - 1)
                wait(dve, s_n[2], g.n - 1)
                dve.tensor_tensor(x2[:, g.par], p_spk[:, 0].rearrange("p (j c) -> p j c", c=C), x1[:, g.par],
                                  ALU.add).then_inc(s_x2, 1)

            def stats_2(g):
                dve.wait_ge(s_x2, g.n + 1)
                statistics(2, g, bn2, x2[:, g.par])

            def moments_2(g):
                wait(dve, s_n[2], g.n)
                moments(2, g, bn2, mv2)

            def mix_2(g, n):
                dve.wait_ge(s_d2, g.n + 1)
                if n:
                    wait(dve, s_fk, HB * g.n)
                else:
                    wait(dve, s_r2, g.n)
                dve.scalar_tensor_tensor(mixed2[:, n], d2[:, :, :], col(("f_tmr", "f_tmk")[n]), z2[:, :, 0:T],
                                         ALU.mult, ALU.add).then_inc(s_mixed2, 1)

            def neuron_input_2(g):
                dve.wait_ge(s_fv, g.n + 1)
                dve.wait_ge(s_tanh_r2, g.n + 1)
                wait(dve, s_spikes[1], g.n)
                dve.scalar_tensor_tensor(flat(h_in[1][:, :, :]), flat(tanh_r2[:, :, :]), 1.0, p_m[0][:, :], ALU.add,
                                         ALU.mult).then_inc(s_h_in[1], 1)

            def add_2(g):
                dve.wait_ge(s_spk_tok[1], g.n + 1)
                wait(dve, s_n[3], g.n)
                dve.tensor_tensor(x3[:, :, :], p_spk[:, 1].rearrange("p (j c) -> p j c", c=C), x2[:, g.par],
                                  ALU.add).then_inc(s_x3, 1)

            def stats_3(g):
                dve.wait_ge(s_x3, g.n + 1)
                statistics(3, g, bn3, x3[:, :, :])

            def moments_3(g):
                wait(dve, s_n[3], g.n)
                moments(3, g, bn3, mv3)

            def stats_4(g):
                dve.wait_ge(s_xres, g.n + 1)
                statistics(4, g, bn4, xres[:, g.par])

            def moments_4(g):
                wait(dve, s_n[4], g.n)
                moments(4, g, bn4, mv4)

            def f0(g):
                dve.wait_ge(s_f0_hi, g.n + 1)
                dve.tensor_tensor(f0_lo[:, 0], p_turn[:, :], f0_hi[:, 0].bitcast(F32),
                                  ALU.subtract).then_inc(s_f0_lo, 1)

            def swiglu(g, m):
                dve.wait_ge(s_ab, 2 * HB * g.n + 2 * m + 2)
                dve.wait_ge(s_gate, HB * g.n + m + 1)
                wait(dve, s_lo[3], (HB - len(POOL_BLOCKS[3])) * g.n)
                wait(dve, s_lo_pool[3], len(POOL_BLOCKS[3]) * g.n)
                if isinstance(g.n, int) and g.n == 0:
                    dve.wait_ge(s_rest, len(parts))
                value = (p_m[1] if m % 2 else p_f[1])[:, :]
                dve.scalar_tensor_tensor(hid[:, m], value, scale[:, 1, m:m + 1], gate[:, m % 2], ALU.mult,
                                         ALU.mult).then_inc(s_swiglu, 1)

            def low(layer, g, m):
                split_low(dve, layer, g, m)

            def stats_5(g):
                dve.wait_ge(s_f_out, g.n + 1)
                statistics(5, g, bn5, f_out[:, :, :])

            def moments_5(g):
                wait(dve, s_n[5], g.n)
                moments(5, g, bn5, mv5)

            def first_turn(pair, step, on):
                nxt, g, c = (Group(pair, step + k) for k in (1, 0, -1))
                if on["shift_k"]:
                    stats_1(nxt)
                    moments_1(nxt)
                if on["wkv"]:
                    terms(g, 0)
                    terms(g, 1)
                    sum_over_time(g, 1)
                    sum_over_time(g, 0)
                if on["shift_k"]:
                    norm_1(nxt)
                if on["wkv"]:
                    denominator(g)
                    numerator(g)
                    ratio(g)
                    ratio_end(g)
                if on["channel"]:
                    neuron_input_2(c)
                    voltage(1, c)
                    fire(1, c)
                if on["weights"]:
                    low_weights(g.n)
                if on["wkv"]:
                    voltage(0, g)
                if on["channel"]:
                    add_2(c)
                if on["wkv"]:
                    fire(0, g)
                if on["channel"]:
                    stats_3(c)
                    moments_3(c)
                if on["shift_k"]:
                    mix_1(nxt, 0)
                    mix_1(nxt, 1)
                if on["wkv"]:
                    add_1(g)
                    stats_2(g)
                    moments_2(g)
                if on["shift_k"]:
                    mix_1(nxt, 2)
                if on["channel"]:
                    stats_4(c)
                    moments_4(c)
                if on["wkv"]:
                    norm_2(g)
                if on["weights"]:
                    count_weights(g.n)
                if on["shift_k"]:
                    maximum(nxt)
                if on["wkv"]:
                    mix_2(g, 0)
                if on["shift_k"]:
                    excess(nxt)
                if on["channel"]:
                    norm_4(c)
                if on["wkv"]:
                    mix_2(g, 1)
                if on["shift_k"]:
                    bounds(nxt, 0)
                    bounds(nxt, 1)
                if on["channel"]:
                    f0(c)
                if on["weights"]:
                    scaled_weights(g.n)

            def turn(pair, step, on):
                nxt, g, c, f, done = (Group(pair, step + k) for k in (1, 0, -1, -2, -3))
                if on["shift_k"]:
                    stats_1(nxt)
                    moments_1(nxt)
                if on["wkv"]:
                    terms(g, 0)
                    terms(g, 1)
                    sum_over_time(g, 1)
                    sum_over_time(g, 0)
                if on["shift_k"]:
                    norm_1(nxt)
                if on["wkv"]:
                    denominator(g)
                if on["store"]:
                    stats_5(done)
                if on["wkv"]:
                    numerator(g)
                if on["store"]:
                    moments_5(done)
                if on["wkv"]:
                    ratio(g)
                    ratio_end(g)
                if on["channel"]:
                    neuron_input_2(c)
                    voltage(1, c)
                if on["ffn"]:
                    swiglu(f, 0)
                if on["channel"]:
                    fire(1, c)
                if on["ffn"]:
                    swiglu(f, 1)
                    low(1, f, 0)
                if on["shift_k"]:
                    mix_1(nxt, 0)
                if on["ffn"]:
                    swiglu(f, 2)
                    swiglu(f, 3)
                    low(1, f, 2)
                    low(1, f, 3)
                if on["wkv"]:
                    voltage(0, g)
                if on["channel"]:
                    add_2(c)
                if on["wkv"]:
                    fire(0, g)
                if on["channel"]:
                    stats_3(c)
                if on["shift_k"]:
                    maximum(nxt)
                if on["channel"]:
                    moments_3(c)
                if on["shift_k"]:
                    mix_1(nxt, 1)
                if on["wkv"]:
                    add_1(g)
                if on["ffn"]:
                    low(2, f, 0)
                if on["wkv"]:
                    stats_2(g)
                    moments_2(g)
                if on["ffn"]:
                    low(2, f, 2)
                    low(2, f, 3)
                if on["shift_k"]:
                    excess(nxt)
                if on["wkv"]:
                    norm_2(g)
                if on["ffn"]:
                    low(3, f, 0)
                if on["shift_k"]:
                    mix_1(nxt, 2)
                if on["channel"]:
                    stats_4(c)
                    moments_4(c)
                if on["wkv"]:
                    mix_2(g, 0)
                    mix_2(g, 1)
                if on["channel"]:
                    norm_4(c)
                if on["shift_k"]:
                    bounds(nxt, 0)
                    bounds(nxt, 1)
                if on["ffn"]:
                    low(3, f, 3)
                if on["channel"]:
                    f0(c)

            def last_turn(pair, step, on):
                c, f, done = (Group(pair, step + k) for k in (-1, -2, -3))
                if on["ffn"]:
                    swiglu(f, 0)
                if on["store"]:
                    stats_5(done)
                if on["ffn"]:
                    swiglu(f, 1)
                if on["store"]:
                    moments_5(done)
                if on["ffn"]:
                    low(1, f, 0)
                    swiglu(f, 2)
                    swiglu(f, 3)
                    low(1, f, 2)
                    low(1, f, 3)
                if on["channel"]:
                    neuron_input_2(c)
                    voltage(1, c)
                    fire(1, c)
                if on["ffn"]:
                    low(2, f, 0)
                if on["channel"]:
                    add_2(c)
                    stats_3(c)
                    moments_3(c)
                if on["ffn"]:
                    low(2, f, 2)
                    low(2, f, 3)
                    low(3, f, 0)
                if on["channel"]:
                    stats_4(c)
                    moments_4(c)
                    norm_4(c)
                if on["ffn"]:
                    low(3, f, 3)
                if on["channel"]:
                    f0(c)

            schedule(dve.Fori, first_turn, turn, last_turn)

        @block.tensor
        def _(pe):
            pe.wait_ge(s_pool_const, 10)
            pe.wait_ge(s_vec, 4)

            def program(general, **turns):
                def turned(n, g, tiles):
                    for j in range(J):
                        last = pe.transpose(p_turn[:, j * P:(j + 1) * P], tiles[:, j], ident[:, :])
                    last.then_inc(s_turned[n], 1)

                def turn_1(g):
                    pe.wait_ge(s_n[1], g.n + 1)
                    wait(pe, s_f0_lo, g.n - 2)
                    wait(pe, s_f_out, g.n - 3)
                    turned(1, g, n1)

                def turn_2(g):
                    pe.wait_ge(s_n[2], g.n + 1)
                    if not isinstance(g.n, int) or g.n + 1 < GROUPS:
                        pe.wait_ge(s_z1, g.n + 2)
                    else:
                        pe.wait_ge(s_f_out, g.n - 2)
                    turned(2, g, n2)

                def turn_4(g):
                    pe.wait_ge(s_n[4], g.n + 1)
                    if not isinstance(g.n, int) or g.n + 1 < GROUPS:
                        pe.wait_ge(s_z2, g.n + 2)
                    else:
                        pe.wait_ge(s_f_out, g.n - 1)
                    turned(4, g, n4)

                def time_product(g, n, name, bank_, done, freed, count):
                    pe.wait_ge(s_mixed1, 3 * g.n + n + 1)
                    if isinstance(g.n, int) and g.n == 0:
                        pe.wait_ge(s_mix_in, 16)
                    for s in freed:
                        wait(pe, s, count)
                    pe.matmul(bank_[:, :], mix[:, MIX[name]], flat(mixed1[:, n]), start=True,
                              stop=True).then_inc(done, 1)

                def k_product(g):
                    time_product(g, 0, "Wk", p_k, s_k, (s_h_in[0],), g.n)

                def v_product(g):
                    wait(pe, s_gate, HB * (g.n - 2))
                    time_product(g, 1, "Wv", p_v, s_v, (s_bv,), 2 * g.n)

                def r_product_1(g):
                    time_product(g, 2, "Wr", p_m[0], s_r, (s_h_in[1],), g.n - 1)

                def out_product(g):
                    pe.wait_ge(s_yr, g.n + 1)
                    pe.wait_ge(s_e, g.n + 1)
                    if isinstance(g.n, int) and g.n == 0:
                        pe.wait_ge(s_quarter, 1)
                    pe.matmul(p_k[:, :], mix[:, MIX["Wo"]], flat(yr[:, :, :]), start=True, stop=True).then_inc(s_wo, 1)

                def spikes_turned(k, g):
                    pe.wait_ge(s_spikes[k], g.n + 1)
                    if k:
                        pe.wait_ge(s_x2, g.n + 1)
                    else:
                        wait(pe, s_x3, g.n)
                    tile = flat(spikes[k][:, :, :])
                    for j in range(J):
                        last = pe.transpose(p_spk[:, k, j * P:(j + 1) * P], tile[:, j * P:(j + 1) * P], ident16[:, :])
                    last.then_inc(s_spk_tok[k], 1)

                def r_product(g):
                    pe.wait_ge(s_mixed2, 2 * g.n + 1)
                    wait(pe, s_relu, HB * g.n)
                    wait(pe, s_swiglu, HB * (g.n - 1))
                    pe.matmul(p_m[1][:, :], mix[:, MIX["fWr"]], flat(mixed2[:, 0]), start=True,
                              stop=True).then_inc(s_r2, 1)

                def channel_k(g, m):
                    if isinstance(g.n, int) and g.n == 0:
                        pe.wait_ge(s_channel_in, 32)
                    pe.wait_ge(s_mixed2, 2 * g.n + 2)
                    if m == 0:
                        if not isinstance(g.n, int) or g.n + 1 < GROUPS:
                            pe.wait_ge(s_tanh_r, g.n + 2)
                        else:
                            pe.wait_ge(s_h_in[1], g.n)
                    elif m == 1:
                        pe.wait_ge(s_tanh_r2, g.n + 1)
                    else:
                        pe.wait_ge(s_relu, HB * g.n + m - 1)
                    pe.matmul(p_m[m % 2][:, :], mix[:, MIX["fWk"] + m], flat(mixed2[:, 1]), start=True,
                              stop=True).then_inc(s_fk, 1)

                def channel_v(g, m):
                    if isinstance(g.n, int) and g.n == 0:
                        pe.wait_ge(s_quarter, 2)
                    if m == 0:
                        pe.wait_ge(s_relu, HB * g.n + HB - 1)
                    pe.wait_ge(s_square, HB * g.n + m + 1)
                    last = pe.matmul(p_m[0][:, :], mix[:, MIX["fWv"] + m], kk[:, m], start=(m == 0),
                                     stop=(m == HB - 1))
                    if m == HB - 1:
                        last.then_inc(s_fv, 1)

                def split_product(out_, blocks, hi, lo, layer=None, g=None):
                    n = len(blocks)
                    for k, b in enumerate(blocks):
                        if layer:
                            pe.wait_ge(s_hi[layer], HB * g.n + k + 1)
                            low_ready(pe, layer, g, k)
                        terms = [(w_hi, lo), (w_hi, hi)] + ([(w_lo, lo), (w_lo, hi)] if general else [])
                        for t, (w, x) in enumerate(terms):
                            last = pe.matmul(out_, w[:, b], x[:, k], start=(k == 0 and t == 0),
                                             stop=(k == n - 1 and t == len(terms) - 1))
                    return last

                def gate_products(g, m):
                    if m == 0:
                        pe.wait_ge(s_f0_hi, g.n + 1)
                        pe.wait_ge(s_f0_lo, g.n + 1)
                        wait(pe, s_f_cm, g.n)
                        wait(pe, s_gelu[2], HB * g.n)
                    elif m == 1:
                        if not isinstance(g.n, int) or g.n + 2 < GROUPS:
                            pe.wait_ge(s_bv, 2 * (g.n + 3))
                        if not isinstance(g.n, int) or g.n + 1 < GROUPS:
                            pe.wait_ge(s_relu, HB * (g.n + 2))
                        wait(pe, s_gate, HB * g.n)
                        wait(pe, s_swiglu, HB * g.n)
                    else:
                        pe.wait_ge(s_gate, HB * g.n + m - 1)
                        pe.wait_ge(s_swiglu, HB * g.n + m - 1)
                    to_gate, to_value = (p_v, p_m[1]) if m % 2 else p_f
                    split_product(to_gate[:, :], [W1 + m], f0_hi, f0_lo).then_inc(s_ab, 1)
                    split_product(to_value[:, :], [W2 + m], f0_hi, f0_lo).then_inc(s_ab, 1)

                def hidden(layer, g, m):
                    if m >= 2:
                        pe.wait_ge(s_gelu[layer], HB * g.n + m - 1)
                    elif layer == 1:
                        pe.wait_ge(s_swiglu, HB * g.n + 3)
                    else:
                        pe.wait_ge(s_gelu[1], HB * g.n + HB - 1 + m)
                    hi, lo = (b_hi, b_lo) if layer == 2 else (ac_hi, ac_lo)
                    first = (H1 if layer == 1 else H2) + m * HB
                    split_product(p_f[m % 2][:, :], range(first, first + HB), hi, lo,
                                  layer if m == 0 else None, g).then_inc(s_h[layer], 1)

                def last_product(g):
                    pe.wait_ge(s_gelu[2], HB * g.n + HB - 1)
                    split_product(p_f[0][:, :], range(W3, W3 + HB), ac_hi, ac_lo, 3, g).then_inc(s_w3, 1)

                def turn_5(g):
                    pe.wait_ge(s_f_cm, g.n + 1)
                    if not isinstance(g.n, int) or g.n + 1 < GROUPS:
                        pe.wait_ge(s_f0_lo, g.n + 2)
                    wait(pe, s_f_out, g.n)
                    for j in range(J):
                        last = pe.transpose(p_turn[:, j * P:(j + 1) * P], f_cm[:, j * P:(j + 1) * P], ident[:, :])
                    last.then_inc(s_turned[5], 1)

                def first_turn(pair, step, on):
                    nxt, g, c = (Group(pair, step + k) for k in (1, 0, -1))
                    if on["channel"]:
                        channel_k(c, 0)
                        channel_k(c, 1)
                        channel_k(c, 2)
                        channel_k(c, 3)
                        channel_v(c, 0)
                        channel_v(c, 1)
                        channel_v(c, 2)
                        channel_v(c, 3)
                    if on["shift_k"]:
                        turn_1(nxt)
                    if on["wkv"]:
                        out_product(g)
                    if on["channel"]:
                        spikes_turned(1, c)
                    if on["wkv"]:
                        spikes_turned(0, g)
                    if on["shift_k"]:
                        k_product(nxt)
                        v_product(nxt)
                        r_product_1(nxt)
                    if on["wkv"]:
                        turn_2(g)
                        r_product(g)
                    if on["channel"]:
                        turn_4(c)

                def turn(pair, step, on):
                    nxt, g, c, f, done = (Group(pair, step + k) for k in (1, 0, -1, -2, -3))
                    if on["channel"]:
                        channel_k(c, 0)
                        channel_k(c, 1)
                    if on["store"]:
                        last_product(done)
                    if on["channel"]:
                        channel_k(c, 2)
                    if on["store"]:
                        turn_5(done)
                    if on["channel"]:
                        channel_k(c, 3)
                        channel_v(c, 0)
                        channel_v(c, 1)
                    if on["shift_k"]:
                        turn_1(nxt)
                    if on["channel"]:
                        channel_v(c, 2)
                        channel_v(c, 3)
                    if on["ffn"]:
                        gate_products(f, 0)
                        gate_products(f, 1)
                    if on["wkv"]:
                        out_product(g)
                    if on["ffn"]:
                        gate_products(f, 2)
                        gate_products(f, 3)
                    if on["shift_k"]:
                        k_product(nxt)
                    if on["channel"]:
                        spikes_turned(1, c)
                    if on["ffn"]:
                        hidden(1, f, 0)
                        hidden(1, f, 1)
                        hidden(1, f, 2)
                    if on["wkv"]:
                        spikes_turned(0, g)
                    if on["ffn"]:
                        hidden(1, f, 3)
                    if on["shift_k"]:
                        v_product(nxt)
                    if on["ffn"]:
                        hidden(2, f, 0)
                        hidden(2, f, 1)
                    if on["wkv"]:
                        turn_2(g)
                    if on["ffn"]:
                        hidden(2, f, 2)
                        hidden(2, f, 3)
                    if on["shift_k"]:
                        r_product_1(nxt)
                    if on["wkv"]:
                        r_product(g)
                    if on["channel"]:
                        turn_4(c)

                def last_turn(pair, step, on):
                    c, f, done = (Group(pair, step + k) for k in (-1, -2, -3))
                    if on["channel"]:
                        channel_k(c, 0)
                        channel_k(c, 1)
                    if on["store"]:
                        last_product(done)
                    if on["channel"]:
                        channel_k(c, 2)
                        channel_k(c, 3)
                    if on["ffn"]:
                        gate_products(f, 0)
                    if on["store"]:
                        turn_5(done)
                    if on["ffn"]:
                        gate_products(f, 1)
                    if on["channel"]:
                        channel_v(c, 0)
                    if on["ffn"]:
                        gate_products(f, 2)
                    if on["channel"]:
                        channel_v(c, 1)
                    if on["ffn"]:
                        gate_products(f, 3)
                    if on["channel"]:
                        channel_v(c, 2)
                        channel_v(c, 3)
                    if on["ffn"]:
                        hidden(1, f, 0)
                        hidden(1, f, 1)
                        hidden(1, f, 2)
                    if on["channel"]:
                        spikes_turned(1, c)
                    if on["ffn"]:
                        hidden(1, f, 3)
                        hidden(2, f, 0)
                        hidden(2, f, 1)
                        hidden(2, f, 2)
                        hidden(2, f, 3)
                    if on["channel"]:
                        turn_4(c)

                schedule(pe.Fori, first_turn, turn, last_turn, **turns)

            program(False, last=1)
            pe.wait_ge(s_hi_w, len(parts))
            pe.wait_ge(s_lo_w, len(parts))
            pe.wait_ge(s_rest_all, 1)
            long_weights = pe.value_load(w_rest_all[0:1, 0:1].bitcast(I32))
            with pe.If(long_weights != 0):
                program(True, first=2)
            with pe.Else():
                program(False, first=2)


def kernel(**inputs):
    import numpy as np
    import concourse.bacc as bacc
    from concourse.bass_utils import run_bass_kernel_spmd

    a = {k[len("L0_attn_"):]: np.asarray(v) for k, v in inputs.items() if k.startswith("L0_attn_")}
    f = {k[len("L0_ffn_"):]: np.asarray(v) for k, v in inputs.items() if k.startswith("L0_ffn_")}
    hb = f["w1_w"].shape[0] // P

    def rows(w):
        return w.reshape(-1, P, w.shape[1]).transpose(1, 0, 2)

    def blocks(w):
        return w.reshape(w.shape[0] // P, P, w.shape[1] // P, P).transpose(3, 0, 2, 1).reshape(P, -1, P)

    arrays = {
        "x": a["x"],
        "vec": np.stack([{**a, **f}[n] for n in VECTORS], axis=1),
        "scale": np.stack([f[n].reshape(hb, P).T for n in ("w1_s", "w2_s", "h1_s", "h2_s")], axis=1),
        "mix": np.concatenate([a[n][:, None, :] for n in ("Wk", "Wv", "Wr", "Wo", "fWr")]
                              + [a["fWk"].reshape(P, hb, P), rows(a["fWv"])], axis=1),
        "ffn": np.concatenate([blocks(f[n]) for n in ("h1_w", "h2_w", "w1_w", "w2_w", "w3_w")], axis=1),
    }
    arrays = {f"in_{k}": np.ascontiguousarray(v) for k, v in arrays.items()}
    nc = bacc.Bacc("TRN2", target_bir_lowering=False, num_devices=1)
    args = [nc.dram_tensor(k, v.shape, mybir.dt.from_np(v.dtype), kind="ExternalInput").ap() for k, v in arrays.items()]
    shape = arrays["in_x"].shape
    out = nc.dram_tensor("out", shape, F32, kind="ExternalOutput").ap()
    build(nc, *args, out)
    r = run_bass_kernel_spmd(nc, [arrays], core_ids=[0])
    return r.results[0]["out"]
```
